# Optimizing a Trainium2 kernel written in Bass

```python
import numpy as np
import jax
import jax.numpy as jnp

def _softmax(x, axis=-1):
    return jax.nn.softmax(x, axis=axis)

def _gelu(x):
    return jax.nn.gelu(x, approximate=True)

def _silu(x):
    return jax.nn.silu(x)

def _sigmoid(x):
    return jax.nn.sigmoid(x)

def _layernorm(x, axis=-1, eps=1e-05):
    m = jnp.mean(x, axis=axis, keepdims=True)
    v = jnp.var(x, axis=axis, keepdims=True)
    return (x - m) / jnp.sqrt(v + eps)

def _scatter_add(tgt, idx, src, axis=0):
    return tgt.at[idx].add(src)

def _segment_sum(src, seg, n):
    return jax.ops.segment_sum(src, seg, n)
kernel_name = 'mk_recurrent_d1_jaxref_r8_60a1fd'

def setup_inputs(seed: int=0):
    np.random.seed(seed)
    _w = jnp.asarray

    def _L0_attn_setup():
        import jax, jax.numpy as jnp
        import numpy as np
        D = 128
        H = 16
        HD = D // H
        EPS = 1e-06

        def rms_norm(x, w):
            xf = x.astype(jnp.float32)
            rms = jnp.sqrt(jnp.mean(xf * xf, axis=-1, keepdims=True) + EPS)
            return (xf / rms * w.astype(jnp.float32)).astype(x.dtype)
        key = jax.random.key(seed)
        ks = jax.random.split(key, 6)
        B, S = (2, 256)
        x = jax.random.normal(ks[0], (B, S, D), dtype=jnp.float32)
        Wqkv = jax.random.normal(ks[1], (3 * D, D), dtype=jnp.float32) * (1.0 / np.sqrt(D))
        bqkv = jax.random.normal(ks[2], (3 * D,), dtype=jnp.float32) * 0.02
        Wproj = jax.random.normal(ks[3], (D, D), dtype=jnp.float32) * (1.0 / np.sqrt(D))
        bproj = jax.random.normal(ks[4], (D,), dtype=jnp.float32) * 0.02
        qn_w = jnp.ones((HD,), dtype=jnp.float32)
        kn_w = jnp.ones((HD,), dtype=jnp.float32)
        return {'x': x, 'Wqkv': Wqkv, 'bqkv': bqkv, 'Wproj': Wproj, 'bproj': bproj, 'qn_w': qn_w, 'kn_w': kn_w}
    _L0_attn_in = _L0_attn_setup()

    def _L0_ffn_setup():
        import jax, jax.numpy as jnp
        import numpy as np
        LN_EPS = 1e-05

        def _layernorm(x, g, b):
            m = jnp.mean(x, axis=-1, keepdims=True)
            v = jnp.mean(jnp.square(x - m), axis=-1, keepdims=True)
            return (x - m) * jax.lax.rsqrt(v + LN_EPS) * g + b
        K_TOP = 2
        key = jax.random.key(seed)
        ks = jax.random.split(key, 4)
        B, N, D, E = (8, 256, 128, 4)
        s = 0.02
        return {'x': jax.random.normal(ks[0], (B, N, D), dtype=jnp.float32), 'gate_W': jax.random.normal(ks[1], (D, E), dtype=jnp.float32) * s, 'gate_b': jnp.zeros((E,), jnp.float32), 'W1': jax.random.normal(ks[2], (E, D, D), dtype=jnp.float32) * s, 'b1': jnp.zeros((E, D), jnp.float32), 'g1': jnp.ones((E, D), jnp.float32), 'be1': jnp.zeros((E, D), jnp.float32), 'W2': jax.random.normal(ks[3], (E, D, D), dtype=jnp.float32) * s, 'b2': jnp.zeros((E, D), jnp.float32), 'g2': jnp.ones((E, D), jnp.float32), 'be2': jnp.zeros((E, D), jnp.float32)}
    _L0_ffn_in = _L0_ffn_setup()
    _d = {'L0_attn_x': _L0_attn_in['x'], 'L0_attn_Wqkv': _L0_attn_in['Wqkv'], 'L0_attn_bqkv': _L0_attn_in['bqkv'], 'L0_attn_Wproj': _L0_attn_in['Wproj'], 'L0_attn_bproj': _L0_attn_in['bproj'], 'L0_attn_qn_w': _L0_attn_in['qn_w'], 'L0_attn_kn_w': _L0_attn_in['kn_w'], 'L0_ffn_gate_W': _L0_ffn_in['gate_W'], 'L0_ffn_gate_b': _L0_ffn_in['gate_b'], 'L0_ffn_W1': _L0_ffn_in['W1'], 'L0_ffn_b1': _L0_ffn_in['b1'], 'L0_ffn_g1': _L0_ffn_in['g1'], 'L0_ffn_be1': _L0_ffn_in['be1'], 'L0_ffn_W2': _L0_ffn_in['W2'], 'L0_ffn_b2': _L0_ffn_in['b2'], 'L0_ffn_g2': _L0_ffn_in['g2'], 'L0_ffn_be2': _L0_ffn_in['be2']}
    _x0 = _d['L0_attn_x']
    _d['L0_attn_x'] = jax.random.normal(jax.random.fold_in(jax.random.key(seed), 1), (2, 1024, 128), dtype=_x0.dtype)
    del _x0
    return _d

def reference(L0_attn_x, L0_attn_Wqkv, L0_attn_bqkv, L0_attn_Wproj, L0_attn_bproj, L0_attn_qn_w, L0_attn_kn_w, L0_ffn_gate_W, L0_ffn_gate_b, L0_ffn_W1, L0_ffn_b1, L0_ffn_g1, L0_ffn_be1, L0_ffn_W2, L0_ffn_b2, L0_ffn_g2, L0_ffn_be2):

    def _L0_attn_ref(x, Wqkv, bqkv, Wproj, bproj, qn_w, kn_w):
        import jax, jax.numpy as jnp
        import numpy as np
        D = 128
        H = 16
        HD = D // H
        EPS = 1e-06

        def rms_norm(x, w):
            xf = x.astype(jnp.float32)
            rms = jnp.sqrt(jnp.mean(xf * xf, axis=-1, keepdims=True) + EPS)
            return (xf / rms * w.astype(jnp.float32)).astype(x.dtype)
        B, S, _ = x.shape
        qkv = x @ Wqkv.T + bqkv
        qkv = qkv.reshape(B, S, 3, H, HD)
        q, k, v = (qkv[:, :, 0], qkv[:, :, 1], qkv[:, :, 2])
        q = rms_norm(q, qn_w)
        k = rms_norm(k, kn_w)
        q = q.transpose(0, 2, 1, 3)
        k = k.transpose(0, 2, 1, 3)
        v = v.transpose(0, 2, 1, 3)
        scale = 1.0 / np.sqrt(HD)
        scores = jnp.einsum('bhsd,bhtd->bhst', q, k) * scale
        attn = jax.nn.softmax(scores, axis=-1)
        out = jnp.einsum('bhst,bhtd->bhsd', attn, v)
        out = out.transpose(0, 2, 1, 3).reshape(B, S, D)
        return out @ Wproj.T + bproj

    def _L0_ffn_ref(x, gate_W, gate_b, W1, b1, g1, be1, W2, b2, g2, be2):
        import jax, jax.numpy as jnp
        import numpy as np
        LN_EPS = 1e-05

        def _layernorm(x, g, b):
            m = jnp.mean(x, axis=-1, keepdims=True)
            v = jnp.mean(jnp.square(x - m), axis=-1, keepdims=True)
            return (x - m) * jax.lax.rsqrt(v + LN_EPS) * g + b
        K_TOP = 2
        B, N, D = x.shape
        BN = B * N
        xf = x.reshape(BN, D)
        gate_scores = xf @ gate_W + gate_b
        topk_scores, topk_idx = jax.lax.top_k(gate_scores, K_TOP)
        weights = jax.nn.softmax(topk_scores, axis=-1)

        def expert(w1, bb1, gg1, bbe1, w2, bb2, gg2, bbe2):
            h = jax.nn.relu(_layernorm(xf @ w1 + bb1, gg1, bbe1))
            return _layernorm(h @ w2 + bb2, gg2, bbe2)
        all_out = jax.vmap(expert)(W1, b1, g1, be1, W2, b2, g2, be2)
        exp_out = all_out[topk_idx, jnp.arange(BN)[:, None]]
        out = jnp.sum(weights[..., None] * exp_out, axis=1)
        return (out + xf).reshape(B, N, D)
    x = L0_attn_x
    xn = _layernorm(x, axis=-1)
    s = _L0_attn_ref(xn, L0_attn_Wqkv, L0_attn_bqkv, L0_attn_Wproj, L0_attn_bproj, L0_attn_qn_w, L0_attn_kn_w)
    g = _silu(_L0_ffn_ref(xn, L0_ffn_gate_W, L0_ffn_gate_b, L0_ffn_W1, L0_ffn_b1, L0_ffn_g1, L0_ffn_be1, L0_ffn_W2, L0_ffn_b2, L0_ffn_g2, L0_ffn_be2))
    x = x + s * g
    return x

_drawn_inputs = setup_inputs


def setup_inputs(seed=0):
    import zlib

    import numpy as np

    out = dict(_drawn_inputs(seed))
    spreads = {'L0_attn_qn_w': (1.0, 0.6),
     'L0_attn_kn_w': (1.0, 0.6),
     'L0_ffn_gate_b': (0.0, 0.298),
     'L0_ffn_b1': (0.0, 0.494),
     'L0_ffn_g1': (1.0, 0.6),
     'L0_ffn_be1': (0.0, 0.8),
     'L0_ffn_b2': (0.0, 0.306),
     'L0_ffn_g2': (1.0, 0.6),
     'L0_ffn_be2': (0.0, 0.8)}
    factors = {'L0_attn_bqkv': 3.137, 'L0_attn_bproj': 3.589}
    for name, (base, spread) in spreads.items():
        noise = np.random.default_rng([zlib.crc32(name.encode()), seed]).standard_normal(out[name].shape)
        drawn = base * np.exp(spread * noise) if base else spread * noise
        out[name] = jnp.asarray(drawn.astype(out[name].dtype))
    for name, factor in factors.items():
        out[name] = (out[name] * factor).astype(out[name].dtype)
    return out
```

```python
from contextlib import ExitStack

import numpy as np

import concourse.bass as bass
from concourse import mybir

F32 = mybir.dt.float32
BFF6 = mybir.dt.bfloat16
I32 = mybir.dt.int32
ALU = mybir.AluOpType
ACT = mybir.ActivationFunctionType
AX_X = mybir.AxisListType.X

P = 128
B, S, D = 2, 1024, 128
H, HD = 16, 8
NE = 4
TOK = B * S
NT = TOK // P
GT = 4
GW = GT * P
NG = TOK // GW
HP = 4
NU = H // HP
KT = S // P
STEPS = 2 * KT
PARTS = 3
QSLOT = 2 * PARTS - 1
QROWS = QSLOT * HD + PARTS
KROWS = PARTS * HD
PAIR = PARTS * KROWS
RING = 8
SBUFS = 3
BLOCK_STEPS = NU * STEPS
SBUF_OF = [k % SBUFS for k in range(BLOCK_STEPS - 1)] + [1]
assert BLOCK_STEPS % SBUFS == 1
QKV = 3 * D
WCAT = QKV + NE
VW = 32
LN_EPS = 1e-5
RMS_EPS = 1e-6
SCALE = HD ** -0.5
EXP_SAFE = 64.0


class Chain:

    def __init__(self, engine, sem, base):
        self.engine, self.sem, self.base, self.n = engine, sem, base, 0

    def link(self, instruction):
        self.n += 1
        instruction.then_inc(self.sem, 1)
        self.engine.wait_ge(self.sem, self.base + self.n)


DVE_PREP = 32
DVE_FIRST = 31
DVE_BLOCK = 44
POOL_PREP = 5
POOL_BLOCK = 16


def build(nc, x, wcat, w1, w2, wproj, row_a, row_b, out):
    with ExitStack() as ctx:
        def sb(name, shape, dt=F32):
            return ctx.enter_context(nc.sbuf_tensor(name, shape, dt))

        def sem(name):
            return ctx.enter_context(nc.semaphore(name))

        q_parts = nc.dram_tensor("q_parts", (H, QROWS, TOK), BFF6).ap()
        k_parts = nc.dram_tensor("k_parts", (H, KROWS, TOK), BFF6).ap()

        wcat_sb = sb("wcat_sb", [P, WCAT])
        w1_sb = sb("w1_sb", [P, NE * D])
        w2_sb = sb("w2_sb", [P, NE * D])
        wproj_sb = sb("wproj_sb", [P, D])
        rowa = sb("rowa", [P, WCAT + 2 * HD])
        rowb = sb("rowb", [P, 6 * NE * D + D])
        E = NE * D
        b1, g1, be1, b2, g2, be2 = (rowb[:, j * E:(j + 1) * E] for j in range(6))
        bproj = rowb[:, 6 * E:6 * E + D]
        ident = sb("ident", [P, P])
        ident16 = sb("ident16", [P, P], BFF6)
        qkw = sb("qkw", [P, 2 * D])

        x_sb = sb("x_sb", [P, NT * D])
        xn = sb("xn", [P, NT * D])
        xnT = sb("xnT", [P, TOK])
        v_sb = sb("v_sb", [P, NT * D])
        gate = sb("gate", [P, NT * D])
        gsc = sb("gsc", [P, NT, NE])
        wgt = sb("wgt", [P, NT * NE])

        stats = sb("stats", [P, GT, 6])
        mv = sb("mv", [P, GT, 2])
        rstd = sb("rstd", [P, GT])
        qk_b = sb("qk_b", [P, GT, 2 * D])
        qk_w = sb("qk_w", [P, GT, 2 * D])
        qk_sq = sb("qk_sq", [P, GT, 2 * D])
        qk_n = sb("qk_n", [P, GT, 2 * D])
        qk_r = sb("qk_r", [P, GT, 2 * D])
        ssum = sb("ssum", [P, GT * 2 * H])
        split = sb("split", [P, PARTS, GT, 2 * D], BFF6)
        splitT = sb("splitT", [P, 2, 2 * PARTS, GW], BFF6)
        zero_rows = sb("zero_rows", [PARTS * H, TOK], BFF6)
        tri = sb("tri", [P, NE, NE])
        cmp_gt = sb("cmp_gt", [P, NT, NE, NE])
        cmp_eq = sb("cmp_eq", [P, NT, NE, NE])
        rank = sb("rank", [P, NT, NE])
        gmax = sb("gmax", [P, NT])
        gexp = sb("gexp", [P, NT, NE])
        gsum = sb("gsum", [P, NT])

        k_op = sb("k_op", [P, 2, HP, S], BFF6)
        q_op = sb("q_op", [P, 2, HP, GW], BFF6)
        v_op = sb("v_op", [P, 2, KT, HP, VW])
        probs = sb("probs", [P, RING, 2 * GW])
        pv_sb = sb("pv_sb", [P, GW])
        rden = sb("rden", [P, GT, HP])
        attn = sb("attn", [P, GT, D])
        attnT = sb("attnT", [P, GW])

        xT_op = sb("xT_op", [P, 2, P])
        h1 = sb("h1", [P, E])
        st1 = sb("st1", [P, NE, 6])
        mv1 = sb("mv1", [P, NE, 2])
        ve1 = sb("ve1", [P, NE])
        rs1 = sb("rs1", [P, NE])
        hn = sb("hn", [P, E])
        hr = sb("hr", [P, E])
        hT = sb("hT", [P, E])
        y = sb("y", [P, E])
        st2 = sb("st2", [P, NE, 6])
        mv2 = sb("mv2", [P, NE, 2])
        ve2 = sb("ve2", [P, NE])
        rs2 = sb("rs2", [P, NE])
        rw2 = sb("rw2", [P, NE])
        z = sb("z", [P, E])
        z2 = sb("z2", [P, E])
        zs = sb("zs", [P, 2 * D])
        moe = sb("moe", [P, D])
        moe_t = sb("moe_t", [P, D])
        neg = sb("neg", [P, D])
        eneg = sb("eneg", [P, D])
        den = sb("den", [P, D])
        sig = sb("sig", [P, D])
        s_t = sb("s_t", [P, D])
        sg = sb("sg", [P, D])
        o_sb = sb("o_sb", [P, 2, D])
        wprod = sb("wprod", [1, HD])
        wmax = sb("wmax", [1, 1])
        large = sb("large", [1, 1], I32)
        smax = sb("smax", [P, NT, H])
        smax_r = sb("smax_r", [P, NT, H])
        smax_q = sb("smax_q", [P, NT, H])
        shift = sb("shift", [P, NT, H, PARTS], BFF6)

        half = sb("half", [P, NE])

        psum = ctx.enter_context(nc.psum_tensor("psum", [P, 8 * 512], F32))

        def bank(n, w=512):
            return psum[:, 512 * n:512 * n + w]

        in_x = [sem(f"in_x{g}") for g in range(NG)]
        in_w = sem("in_w")
        in_wb = sem("in_wb")
        ident_ready = sem("ident_ready")
        cleared = sem("cleared")
        dve_links = sem("dve_links")
        pool_links = sem("pool_links")
        dve_waits = sem("dve_waits")
        pool_waits = sem("pool_waits")
        lnvar_ready = sem("lnvar_ready")
        lnstd_ready = sem("lnstd_ready")
        xn_ready = sem("xn_ready")
        xT_done = sem("xT_done")
        xnT_ready = sem("xnT_ready")
        qkv_done = sem("qkv_done")
        qkv_taken = sem("qkv_taken")
        qk_ready = sem("qk_ready")
        sq_ready = sem("sq_ready")
        ms_ready = sem("ms_ready")
        rms_ready = sem("rms_ready")
        qkw_ready = sem("qkw_ready")
        qkn_ready = sem("qkn_ready")
        hi_ready = sem("hi_ready")
        res_ready = sem("res_ready")
        mid_ready = sem("mid_ready")
        lo_ready = sem("lo_ready")
        partsT_done = sem("partsT_done")
        partsT_dve = sem("partsT_dve")
        partsT_act = sem("partsT_act")
        stored = [sem(f"stored{g}") for g in range(2)]
        shift_zeroed = sem("shift_zeroed")
        gdiff_ready = sem("gdiff_ready")
        gexp_ready = sem("gexp_ready")
        wgt_ready = sem("wgt_ready")

        large_ready = sem("large_ready")
        max_operands_in = sem("max_operands_in")
        max_scores_done = sem("max_scores_done")
        max_taken = sem("max_taken")
        max_links = sem("max_links")
        shift_ready = sem("shift_ready")
        shiftT_done = sem("shiftT_done")
        shift_rows_ready = sem("shift_rows_ready")
        shift_stored = sem("shift_stored")

        operands_in = [sem(f"operands_in{j}") for j in range(2)]
        scores_done = sem("scores_done")
        probs_ready = sem("probs_ready")
        pv_done = sem("pv_done")
        staged = sem("staged")
        pv_taken = sem("pv_taken")
        pvT_done = sem("pvT_done")
        attn_ready = sem("attn_ready")
        attnT_done = sem("attnT_done")
        attnT_ready = sem("attnT_ready")
        mm1_done = sem("mm1_done")
        h1_taken = sem("h1_taken")
        mv1_ready = sem("mv1_ready")
        rs1_ready = sem("rs1_ready")
        hn_ready = sem("hn_ready")
        hg_ready = sem("hg_ready")
        hr_ready = sem("hr_ready")
        hT_done = sem("hT_done")
        hT_ready = sem("hT_ready")
        mm2_done = sem("mm2_done")
        y_taken = sem("y_taken")
        mv2_ready = sem("mv2_ready")
        rs2_ready = sem("rs2_ready")
        z_ready = sem("z_ready")
        zg_ready = sem("zg_ready")
        neg_ready = sem("neg_ready")
        eneg_ready = sem("eneg_ready")
        proj_done = sem("proj_done")
        proj_taken = sem("proj_taken")
        out_ready = sem("out_ready")
        out_stored = [sem(f"out_stored{j}") for j in range(2)]

        x_v = x.rearrange("b (t p) d -> p (b t) d", p=P)
        out_v = out.rearrange("b (t p) d -> p (b t) d", p=P)
        x_3 = x_sb[:, :].rearrange("p (t d) -> p t d", d=D)
        qkv_ps = psum[:, 512:512 * 5].rearrange("p (t c) -> p t c", t=GT)
        parts_ps = psum[:, 512 * 5:512 * 8].bitcast(BFF6).rearrange("p (s t c) -> p s t c", s=2 * PARTS, t=GT)
        PV, FF = bank(6), bank(7)

        MAXN = HP * GT
        CREDIT = 2

        def scores_may_be_large(engine):
            engine.wait_ge(large_ready, 1)
            return engine.value_load(large[0:1, 0:1], min_val=0, max_val=1) > 0

        block = ctx.enter_context(nc.Block())

        @block.sync
        def _(sp):
            sp.dma_start(x_3[:, 0:GT, :], x_v[:, 0:GT, :]).then_inc(in_x[0], 16)
            sp.dma_start(wcat_sb[:, :], wcat).then_inc(in_w, 16)
            sp.dma_start(rowa[:, :], row_a.broadcast_to([P, WCAT + 2 * HD])).then_inc(in_w, 16)
            for g in range(1, NG):
                sp.dma_start(x_3[:, GT * g:GT * (g + 1), :], x_v[:, GT * g:GT * (g + 1), :]).then_inc(in_x[g], 16)
            sp.dma_start(w1_sb[:, :], w1).then_inc(in_wb, 16)
            sp.dma_start(w2_sb[:, :], w2).then_inc(in_wb, 16)
            sp.dma_start(wproj_sb[:, :], wproj).then_inc(in_wb, 16)
            sp.dma_start(rowb[:, :], row_b.broadcast_to([P, 6 * E + D])).then_inc(in_wb, 16)
            sp.wait_ge(cleared, 1)
            sp.dma_start(q_parts[:, QSLOT * HD:, :], zero_rows[:, :]).then_inc(shift_zeroed, 16)
            for g in range(NG):
                cols = slice(GW * g, GW * (g + 1))
                sp.wait_ge(partsT_dve, g + 1)
                sp.wait_ge(partsT_act, g + 1)
                for slot in range(QSLOT):
                    sp.dma_start(q_parts[:, slot * HD:(slot + 1) * HD, cols],
                                 splitT[:, g % 2, slot % PARTS, :]).then_inc(stored[g % 2], 16)
                for part in range(PARTS):
                    sp.dma_start(k_parts[:, part * HD:(part + 1) * HD, cols],
                                 splitT[:, g % 2, PARTS + part, :]).then_inc(stored[g % 2], 16)

            def operand_dmas(i, u, par, arrived):
                for a in range(PARTS):
                    sp.dma_start(k_op[KROWS * a:KROWS * (a + 1), par, :, :],
                                 k_parts[HP * u:HP * (u + 1), :, bass.ds((i // 2) * S, S)]
                                 .rearrange("h r t -> r h t")).then_inc(arrived, 16)
                    rows = KROWS + (PARTS if a == PARTS - 1 else 0)
                    sp.dma_start(q_op[KROWS * a:KROWS * a + rows, par, :, :],
                                 q_parts[HP * u:HP * (u + 1), HD * a:HD * a + rows, bass.ds(i * GW, GW)]
                                 .rearrange("h r t -> r h t")).then_inc(arrived, 16)

            def load_operands(i, u, first):
                par = u % 2
                if not (first and u < 2):
                    sp.wait_ge(scores_done, i * NU * STEPS + STEPS * (u - 1))
                operand_dmas(i, u, par, operands_in[par])

            def store_tile(i, u, count):
                sp.wait_ge(out_ready, count)
                sp.dma_start(out_v[:, bass.ds(i * GT + u, 1), :], o_sb[:, u % 2:u % 2 + 1, :]).then_inc(
                    out_stored[u % 2], 16)

            for par in range(2):
                sp.wait_ge(stored[par], 16 * (QSLOT + PARTS) * NG // 2)
            sp.wait_ge(shift_zeroed, 16)
            sp.wait_ge(cleared, 3)
            with sp.If(scores_may_be_large(sp)):
                with sp.Fori(0, NG) as i:
                    for u in range(NU):
                        sp.wait_ge(max_taken, (i * NU + u) * MAXN + CREDIT)
                        operand_dmas(i, u, 0, max_operands_in)
                sp.wait_ge(shift_rows_ready, 1)
                sp.dma_start(q_parts[:, QSLOT * HD:, :], zero_rows[:, :]).then_inc(shift_stored, 16)
                sp.wait_ge(shift_stored, 16)
            for u in range(NU):
                load_operands(0, u, True)
            for u in range(NU):
                if u >= 2:
                    store_tile(0, u - 2, u - 1)
                load_operands(1, u, False)
            with sp.Fori(2, NG) as i:
                for u in range(NU):
                    store_tile(i - 2 if u < 2 else i - 1, (u - 2) % NU, (i - 2) * GT + u + 3)
                    load_operands(i, u, False)
            for t in range(NT - GT - 2, NT):
                store_tile(t // GT, t % GT, t + 1)
            for par in range(2):
                sp.wait_ge(out_stored[par], 16 * NT // 2)

        @block.gpsimd
        def _(pool):
            gp = nc.gpsimd
            ch = Chain(pool, pool_links, 0)
            ch.link(gp.memset(ident[:], 0.0))
            ch.link(gp.affine_select(out=ident[:, :], in_=ident[:, :], compare_op=ALU.not_equal, fill=1.0,
                                     base=0, pattern=[[-1, P]], channel_multiplier=1))
            gp.tensor_copy(ident16[:, :], ident[:, :]).then_inc(ident_ready, 1)
            gp.memset(zero_rows[:], 0.0).then_inc(cleared, 1)
            pool.wait_ge(cleared, 1)
            gp.memset(q_op[:], 0.0).then_inc(cleared, 1)
            pool.wait_ge(cleared, 2)
            gp.memset(k_op[:], 1.0).then_inc(cleared, 1)
            gp.memset(half[:], -0.5)
            ch.link(gp.memset(v_op[:], 0.0))
            ch.link(gp.memset(v_op[:, :, :, :, HD:HD + 1], 1.0))
            pool.wait_ge(in_w, 32)
            qn = rowa[:, WCAT:WCAT + HD]
            kn = rowa[:, WCAT + HD:WCAT + 2 * HD]
            gp.tensor_scalar(qkw[:, 0:D].rearrange("p (h d) -> p h d", d=HD),
                             qn.unsqueeze(1).broadcast_to([P, H, HD]), SCALE, 1.0, ALU.mult, ALU.mult)
            ch.link(gp.tensor_scalar(qkw[:, D:2 * D].rearrange("p (h d) -> p h d", d=HD),
                                     kn.unsqueeze(1).broadcast_to([P, H, HD]), 1.0, 1.0, ALU.mult, ALU.mult))
            for g in range(NG):
                pool.wait_ge(qk_ready, g + 1)
                if g:
                    pool.wait_ge(qkn_ready, g)
                gp.tensor_tensor(qk_w[:, :, :], qk_b[:, :, :],
                                 qkw[:, :].unsqueeze(1).broadcast_to([P, GT, 2 * D]), ALU.mult).then_inc(qkw_ready, 1)
            assert ch.n == POOL_PREP, ("POOL_PREP", ch.n)

            def stage(i, u):
                pool.sem_inc(pool_waits, 1)
                v_b = v_sb[:, bass.ds((i // 2) * (KT * D), KT * D)].rearrange("p (t c) -> p t c", c=D)
                gp.tensor_copy(v_op[:, u % 2, :, :, 0:HD],
                               v_b[:, :, HP * HD * u:HP * HD * (u + 1)].rearrange("p t (h d) -> p t h d", d=HD)
                               ).then_inc(staged, 1)
                gp.tensor_copy(xT_op[:, u % 2, :], xnT[:, bass.ds(i * GW + u * P, P)]).then_inc(staged, 1)

            def power(ch, dst, tmp, mv_):
                pool.sem_inc(pool_waits, 1)
                ch.link(gp.tensor_scalar(tmp[:, :], mv_[:, :, 1], LN_EPS, 1.0, ALU.add, ALU.mult))
                return gp.tensor_tensor(dst[:, :], tmp[:, :], half[:, :], ALU.pow)

            def experts_b(i, u, ch, prev):
                pool.wait_ge(mv2_ready, prev)
                ch.link(power(ch, rs2, ve2, mv2))
                gp.tensor_tensor(rw2[:, :], rs2[:, :], wgt[:, bass.ds((i * NU + u) * NE, NE)],
                                 ALU.mult).then_inc(rs2_ready, 1)

            def scale_b(prev):
                pool.wait_ge(z_ready, prev)
                gp.tensor_tensor(z2[:, :], z[:, :], g2, ALU.mult).then_inc(zg_ready, 1)

            def one_block(i, ch, first):
                for u in range(NU):
                    n = i * NU + u
                    if not (first and u == 0):
                        experts_b(i if u else i - 1, (u - 1) % NU, ch, n)
                    if not (first and u == 0):
                        pool.wait_ge(pv_done, i * NU * KT + KT * u)
                    stage(i if u < NU - 1 else i + 1, (u + 1) % NU)
                    pool.wait_ge(mv1_ready, n + 1)
                    power(ch, rs1, ve1, mv1).then_inc(rs1_ready, 1)
                    if not (first and u == 0):
                        scale_b(n)
                    pool.wait_ge(hn_ready, n + 1)
                    ch.link(gp.tensor_tensor(hn[:, :], hn[:, :], g1, ALU.mult))
                    gp.tensor_tensor(hn[:, :], hn[:, :], be1, ALU.add).then_inc(hg_ready, 1)

            pool.wait_ge(qkv_taken, NG)
            pool.wait_ge(xnT_ready, NG)
            stage(0, 0)
            pool.wait_ge(in_wb, 64)
            pool.wait_ge(wgt_ready, 1)
            c0 = Chain(pool, pool_links, POOL_PREP)
            one_block(0, c0, True)
            assert c0.n == POOL_BLOCK - 2, ("POOL_BLOCK", c0.n + 2)
            with pool.Fori(1, NG - 1) as i:
                ci = Chain(pool, pool_links, (i - 1) * POOL_BLOCK + (POOL_PREP + POOL_BLOCK - 2))
                one_block(i, ci, False)
                assert ci.n == POOL_BLOCK, ("POOL_BLOCK", ci.n)
            cl = Chain(pool, pool_links, POOL_PREP + (NG - 1) * POOL_BLOCK - 2)
            last = NG - 1
            for u in range(NU):
                n = last * NU + u
                experts_b(last if u else last - 1, (u - 1) % NU, cl, n)
                if u < NU - 1:
                    pool.wait_ge(pv_done, last * NU * KT + KT * u)
                    stage(last, u + 1)
                pool.wait_ge(mv1_ready, n + 1)
                power(cl, rs1, ve1, mv1).then_inc(rs1_ready, 1)
                scale_b(n)
                pool.wait_ge(hn_ready, n + 1)
                cl.link(gp.tensor_tensor(hn[:, :], hn[:, :], g1, ALU.mult))
                gp.tensor_tensor(hn[:, :], hn[:, :], be1, ALU.add).then_inc(hg_ready, 1)
            experts_b(last, NU - 1, cl, NT)
            scale_b(NT)

        @block.scalar
        def _(act):
            sc = nc.scalar

            def ln_std(g):
                act.wait_ge(lnvar_ready, g + 1)
                sc.activation(rstd[:, :], rstd[:, :], ACT.Sqrt).then_inc(lnstd_ready, 1)

            def copy_xT(g):
                act.wait_ge(xT_done, g + 1)
                sc.activation(xnT[:, GW * g:GW * (g + 1)], bank(0), ACT.Copy).then_inc(xnT_ready, 1)

            ln_std(0)
            copy_xT(0)
            for g in range(NG):
                act.wait_ge(qk_ready, g + 1)
                sc.activation(qk_sq[:, :, :], qk_b[:, :, :], ACT.Square).then_inc(sq_ready, 1)
                if g + 1 < NG:
                    ln_std(g + 1)
                act.wait_ge(ms_ready, g + 1)
                sc.activation(ssum[:, :], ssum[:, :], ACT.Sqrt).then_inc(rms_ready, 1)
                if g + 1 < NG:
                    copy_xT(g + 1)
                act.wait_ge(qkn_ready, g + 1)
                if g:
                    act.wait_ge(partsT_done, g)
                sc.activation(split[:, 0, :, :], qk_n[:, :, :], ACT.Copy).then_inc(hi_ready, 1)
                act.wait_ge(res_ready, g + 1)
                sc.activation(split[:, 1, :, :], qk_r[:, :, :], ACT.Copy).then_inc(mid_ready, 1)
                act.wait_ge(partsT_done, g + 1)
                if g >= 2:
                    act.wait_ge(stored[g % 2], 16 * (QSLOT + PARTS) * (g // 2))
                sc.activation(splitT[:, g % 2, 0:2, :], parts_ps[:, 0:2, :, :], ACT.Copy).then_inc(partsT_act, 1)
            act.wait_ge(gdiff_ready, 1)
            sc.activation(gexp[:, :, :], gexp[:, :, :], ACT.Exp).then_inc(gexp_ready, 1)

            def exp_step(i, k, first):
                n = i * NU * STEPS + k
                act.wait_ge(scores_done, n + 1)
                if not (first and k < RING):
                    act.wait_ge(pv_done, i * NU * KT + (k - RING) // 2 + 1)
                sc.activation(probs[:, k % RING, :], bank(2 * SBUF_OF[k], 2 * GW),
                              ACT.Exp).then_inc(probs_ready, 1)

            def exp_neg(count):
                act.wait_ge(neg_ready, count)
                sc.activation(eneg[:, :], neg[:, :], ACT.Exp).then_inc(eneg_ready, 1)

            def one_block(i, first):
                for u in range(NU):
                    for k in range(STEPS):
                        exp_step(i, u * STEPS + k, first)
                        if k == STEPS - 2 and not (first and u == 0):
                            exp_neg(i * NU + u)

            one_block(0, True)
            with act.Fori(1, NG) as i:
                one_block(i, False)
            exp_neg(NT)

        @block.vector
        def _(dve):
            ve = nc.vector
            ch = Chain(dve, dve_links, 0)

            def ln_stats(g):
                dve.wait_ge(in_x[g], 16)
                for u in range(GT):
                    st = ve.bn_stats(stats[:, u, :], x_3[:, GT * g + u, :])
                ch.link(st)
                for u in range(GT):
                    st = ve.bn_aggr(mv[:, u, :], stats[:, u, :])
                ch.link(st)
                ve.tensor_scalar(rstd[:, :], mv[:, :, 1], LN_EPS, None, ALU.add).then_inc(lnvar_ready, 1)

            def ln_apply(g):
                dve.wait_ge(lnstd_ready, g + 1)
                ch.link(ve.reciprocal(rstd[:, :], rstd[:, :]))
                for u in range(GT):
                    t = GT * g + u
                    last = ve.tensor_scalar(xn[:, D * t:D * (t + 1)], x_sb[:, D * t:D * (t + 1)], mv[:, u, 0:1],
                                            rstd[:, u:u + 1], ALU.subtract, ALU.mult)
                last.then_inc(xn_ready, 1)

            bias = rowa[:, 0:WCAT]
            for e in range(1, NE):
                ve.memset(tri[:, e, 0:e], 1.0)
            for e in range(NE):
                st = ve.memset(tri[:, e, e:NE], 0.0)
            ch.link(st)
            ln_stats(0)
            ln_apply(0)
            dve.wait_ge(in_w, 32)
            ch.link(ve.tensor_tensor(wprod[:, :], rowa[0:1, WCAT:WCAT + HD], rowa[0:1, WCAT + HD:WCAT + 2 * HD],
                                     ALU.mult))
            ch.link(ve.tensor_tensor(wprod[:, :], wprod[:, :], wprod[:, :], ALU.mult))
            ch.link(ve.tensor_reduce(wmax[:, :], wprod[:, :], AX_X, ALU.max))
            ve.tensor_scalar(large[:, :], wmax[:, :], (EXP_SAFE / (SCALE * HD)) ** 2, None,
                             ALU.is_gt).then_inc(large_ready, 1)
            for g in range(NG):
                dve.wait_ge(in_w, 32)
                dve.wait_ge(qkv_done, g + 1)
                if g:
                    dve.wait_ge(qkw_ready, g)
                    dve.wait_ge(sq_ready, g)
                ve.tensor_tensor(qk_b[:, :, :], qkv_ps[:, :, 0:2 * D],
                                 bias[:, 0:2 * D].unsqueeze(1).broadcast_to([P, GT, 2 * D]),
                                 ALU.add).then_inc(qk_ready, 1)
                ve.tensor_tensor(v_sb[:, GW * g:GW * (g + 1)].rearrange("p (t c) -> p t c", t=GT),
                                 qkv_ps[:, :, 2 * D:QKV],
                                 bias[:, 2 * D:QKV].unsqueeze(1).broadcast_to([P, GT, D]), ALU.add)
                ve.tensor_tensor(gsc[:, GT * g:GT * (g + 1), :], qkv_ps[:, :, QKV:WCAT],
                                 bias[:, QKV:WCAT].unsqueeze(1).broadcast_to([P, GT, NE]),
                                 ALU.add).then_inc(qkv_taken, 1)
                dve.wait_ge(sq_ready, g + 1)
                ch.link(ve.tensor_reduce(ssum[:, :], qk_sq[:, :, :].rearrange("p t (h d) -> p (t h) d", d=HD),
                                         AX_X, ALU.add))
                ve.tensor_scalar(ssum[:, :], ssum[:, :], 1.0 / HD, RMS_EPS, ALU.mult, ALU.add).then_inc(ms_ready, 1)
                if g + 1 < NG:
                    ln_stats(g + 1)
                dve.wait_ge(rms_ready, g + 1)
                ch.link(ve.reciprocal(ssum[:, :], ssum[:, :]))
                dve.wait_ge(qkw_ready, g + 1)
                ve.tensor_tensor(qk_n[:, :, :].rearrange("p t (h d) -> p (t h) d", d=HD),
                                 qk_w[:, :, :].rearrange("p t (h d) -> p (t h) d", d=HD),
                                 ssum[:, :].unsqueeze(2).broadcast_to([P, GT * 2 * H, HD]),
                                 ALU.mult).then_inc(qkn_ready, 1)
                if g + 1 < NG:
                    ln_apply(g + 1)
                dve.wait_ge(hi_ready, g + 1)
                ve.tensor_tensor(qk_r[:, :, :], qk_n[:, :, :], split[:, 0, :, :], ALU.subtract).then_inc(res_ready, 1)
                dve.wait_ge(mid_ready, g + 1)
                ve.tensor_tensor(split[:, 2, :, :], qk_r[:, :, :], split[:, 1, :, :],
                                 ALU.subtract).then_inc(lo_ready, 1)
                dve.wait_ge(partsT_done, g + 1)
                if g >= 2:
                    dve.wait_ge(stored[g % 2], 16 * (QSLOT + PARTS) * (g // 2))
                ve.tensor_copy(splitT[:, g % 2, 2:6, :], parts_ps[:, 2:6, :, :]).then_inc(partsT_dve, 1)

            of_f = gsc[:, :, :].unsqueeze(2).broadcast_to([P, NT, NE, NE])
            of_e = gsc[:, :, :].unsqueeze(3).broadcast_to([P, NT, NE, NE])
            flat = "p t e f -> p t (e f)"
            dve.wait_ge(qkv_taken, NG)
            ve.tensor_reduce(gmax[:, :], gsc[:, :, :], AX_X, ALU.max)
            ve.tensor_tensor(cmp_gt[:, :, :, :], of_f, of_e, ALU.is_gt)
            ch.link(ve.tensor_tensor(cmp_eq[:, :, :, :], of_f, of_e, ALU.is_equal))
            ve.tensor_tensor(gexp[:, :, :], gsc[:, :, :], gmax[:, :].unsqueeze(2).broadcast_to([P, NT, NE]),
                             ALU.subtract).then_inc(gdiff_ready, 1)
            ch.link(ve.tensor_tensor(cmp_eq[:, :, :, :].rearrange(flat), cmp_eq[:, :, :, :].rearrange(flat),
                                     tri[:, :, :].rearrange("p e f -> p (e f)").unsqueeze(1)
                                     .broadcast_to([P, NT, NE * NE]), ALU.mult))
            ch.link(ve.tensor_tensor(cmp_gt[:, :, :, :], cmp_gt[:, :, :, :], cmp_eq[:, :, :, :], ALU.add))
            ch.link(ve.tensor_reduce(rank[:, :, :], cmp_gt[:, :, :, :], AX_X, ALU.add))
            ch.link(ve.tensor_scalar(rank[:, :, :], rank[:, :, :], 1.5, None, ALU.is_lt))
            dve.wait_ge(gexp_ready, 1)
            ch.link(ve.tensor_tensor(gexp[:, :, :], gexp[:, :, :], rank[:, :, :], ALU.mult))
            ch.link(ve.tensor_reduce(gsum[:, :], gexp[:, :, :], AX_X, ALU.add))
            ch.link(ve.reciprocal(gsum[:, :], gsum[:, :]))
            ve.tensor_tensor(wgt[:, :].rearrange("p (t e) -> p t e", e=NE), gexp[:, :, :],
                             gsum[:, :].unsqueeze(2).broadcast_to([P, NT, NE]), ALU.mult).then_inc(wgt_ready, 1)
            dve.wait_ge(wgt_ready, 1)
            dve.wait_ge(in_wb, 64)
            assert ch.n == DVE_PREP, ("DVE_PREP", ch.n)

            with dve.If(scores_may_be_large(dve)):
                dve.sem_inc(max_taken, CREDIT)
                with dve.Fori(0, NG) as i:
                    for u in range(NU):
                        for m in range(MAXN):
                            head, q = HP * u + m // GT, m % GT
                            dve.wait_ge(max_scores_done, (i * NU + u) * MAXN + m + 1)
                            dve.sem_inc(dve_waits, 1)
                            ve.tensor_reduce(smax[:, bass.ds(i * GT + q, 1), head], bank(2 * (m % 2), 2 * GW),
                                             AX_X, ALU.max).then_inc(max_taken, 1)
                dve.wait_ge(max_taken, NG * NU * MAXN + CREDIT)
                cm = Chain(dve, max_links, 0)
                cm.link(ve.tensor_scalar(smax_r[:, :, :], smax[:, :, :], -1.0, None, ALU.mult))
                cm.link(ve.tensor_copy(shift[:, :, :, 0], smax_r[:, :, :]))
                cm.link(ve.tensor_tensor(smax_q[:, :, :], smax_r[:, :, :], shift[:, :, :, 0], ALU.subtract))
                cm.link(ve.tensor_copy(shift[:, :, :, 1], smax_q[:, :, :]))
                ve.tensor_tensor(shift[:, :, :, 2], smax_q[:, :, :], shift[:, :, :, 1],
                                 ALU.subtract).then_inc(shift_ready, 1)
                dve.wait_ge(shiftT_done, 1)
                dve.wait_ge(shift_zeroed, 16)
                ve.tensor_copy(zero_rows[:, :], psum[0:H * PARTS, 0:2 * GW].bitcast(BFF6)).then_inc(shift_rows_ready, 1)

            def col(e):
                return slice(D * e, D * (e + 1))

            def take_y(n_done, ch):
                dve.wait_ge(mm2_done, n_done)
                ve.tensor_tensor(y[:, :], FF, b2, ALU.add).then_inc(y_taken, 1)
                dve.wait_ge(y_taken, n_done)
                for e in range(NE):
                    st = ve.bn_stats(st2[:, e, :], y[:, col(e)])
                ch.link(st)
                dve.sem_inc(dve_waits, 1)
                for e in range(NE):
                    st = ve.bn_aggr(mv2[:, e, :], st2[:, e, :])
                st.then_inc(mv2_ready, 1)

            def take_h(n_done, ch):
                dve.wait_ge(mm1_done, n_done)
                ve.tensor_tensor(h1[:, :], FF, b1, ALU.add).then_inc(h1_taken, 1)
                dve.wait_ge(h1_taken, n_done)
                for e in range(NE):
                    st = ve.bn_stats(st1[:, e, :], h1[:, col(e)])
                ch.link(st)
                dve.sem_inc(dve_waits, 1)
                for e in range(NE):
                    st = ve.bn_aggr(mv1[:, e, :], st1[:, e, :])
                st.then_inc(mv1_ready, 1)

            def normalize(dst, src, mv_, rs, done):
                for e in range(NE):
                    st = ve.tensor_scalar(dst[:, col(e)], src[:, col(e)], mv_[:, e, 0:1], rs[:, e:e + 1],
                                          ALU.subtract, ALU.mult)
                st.then_inc(done, 1)

            def scale_y(n_done):
                dve.wait_ge(rs2_ready, n_done)
                normalize(z, y, mv2, rw2, z_ready)

            def mix(i, u, n_done, ch):
                t = i * NU + u
                dve.wait_ge(zg_ready, n_done)
                for e in range(NE):
                    st = ve.scalar_tensor_tensor(z[:, col(e)], be2[:, col(e)], wgt[:, bass.ds(t * NE + e, 1)],
                                                 z2[:, col(e)], ALU.mult, ALU.add)
                ch.link(st)
                ch.link(ve.tensor_tensor(zs[:, :], z[:, 0:2 * D], z[:, 2 * D:4 * D], ALU.add))
                ch.link(ve.tensor_tensor(moe_t[:, :], zs[:, 0:D], zs[:, D:2 * D], ALU.add))
                ch.link(ve.tensor_tensor(moe[:, :], moe_t[:, :], xn[:, bass.ds(t * D, D)], ALU.add))
                ve.tensor_scalar(neg[:, :], moe[:, :], -1.0, 87.0, ALU.mult, ALU.min).then_inc(neg_ready, 1)

            def silu(i, u, n_done, ch):
                dve.wait_ge(eneg_ready, n_done)
                ch.link(ve.tensor_scalar(den[:, :], eneg[:, :], 1.0, None, ALU.add))
                ch.link(ve.reciprocal(sig[:, :], den[:, :]))
                ch.link(ve.tensor_tensor(gate[:, bass.ds((i * NU + u) * D, D)], moe[:, :], sig[:, :], ALU.mult))

            def take_pv(passes):
                dve.wait_ge(pv_done, KT * passes)
                ve.tensor_copy(pv_sb[:, :], PV).then_inc(pv_taken, 1)

            def divide(passes, u, ch):
                dve.wait_ge(pvT_done, passes)
                pvT = FF.rearrange("p (q h c) -> p q h c", q=GT, h=HP)
                ch.link(ve.reciprocal(rden[:, :, :], pvT[:, :, :, HD]))
                ve.tensor_tensor(attn[:, :, HP * HD * u:HP * HD * (u + 1)].rearrange("p q (h d) -> p q h d", d=HD),
                                 pvT[:, :, :, 0:HD], rden[:, :, :].unsqueeze(3).broadcast_to([P, GT, HP, HD]),
                                 ALU.mult).then_inc(attn_ready, 1)

            def take_attnT(blocks):
                dve.wait_ge(attnT_done, blocks)
                ve.tensor_copy(attnT[:, :], FF).then_inc(attnT_ready, 1)

            def relu(n_done):
                dve.wait_ge(hg_ready, n_done)
                ve.tensor_scalar(hr[:, :], hn[:, :], 0.0, None, ALU.max).then_inc(hr_ready, 1)

            def take_hT(n_done):
                dve.wait_ge(hT_done, n_done)
                ve.tensor_copy(hT[:, :], FF).then_inc(hT_ready, 1)

            def finish(i, u, n_done, ch, reuse):
                t = i * GT + u
                dve.wait_ge(proj_done, n_done)
                ve.tensor_tensor(s_t[:, :], FF[:, 0:D], bproj, ALU.add).then_inc(proj_taken, 1)
                dve.wait_ge(proj_taken, n_done)
                ch.link(ve.tensor_tensor(sg[:, :], s_t[:, :], gate[:, bass.ds(t * D, D)], ALU.mult))
                if reuse is not None:
                    dve.wait_ge(out_stored[u % 2], reuse)
                ve.tensor_tensor(o_sb[:, u % 2, :], sg[:, :], x_sb[:, bass.ds(t * D, D)], ALU.add).then_inc(out_ready, 1)

            def one_block(i, ch, first, second):
                for u in range(NU):
                    n = i * NU + u
                    head = first and u == 0
                    before = (i if u else i - 1, (u - 1) % NU)
                    if not head:
                        take_pv(n)
                        take_y(n, ch)
                    take_h(n + 1, ch)
                    if not head:
                        scale_y(n)
                    dve.wait_ge(rs1_ready, n + 1)
                    normalize(hn, h1, mv1, rs1, hn_ready)
                    if not head:
                        divide(n, (u - 1) % NU, ch)
                        mix(*before, n, ch)
                    if u == 0 and not first:
                        take_attnT(i)
                    relu(n + 1)
                    if not first:
                        early = second and u < 2
                        finish(i - 1, u, n - NU + 1, ch, None if early else (i - 1) * (16 * GT // 2) + 16 * (u // 2))
                    take_hT(n + 1)
                    if not head:
                        silu(*before, n, ch)

            c0 = Chain(dve, dve_links, DVE_PREP)
            one_block(0, c0, True, False)
            assert c0.n == DVE_FIRST, ("DVE_FIRST", c0.n)
            c1 = Chain(dve, dve_links, DVE_PREP + DVE_FIRST)
            one_block(1, c1, False, True)
            assert c1.n == DVE_BLOCK, ("DVE_BLOCK", c1.n)
            with dve.Fori(2, NG) as i:
                ci = Chain(dve, dve_links, (i - 2) * DVE_BLOCK + (DVE_PREP + DVE_FIRST + DVE_BLOCK))
                one_block(i, ci, False, False)
            ce = Chain(dve, dve_links, DVE_PREP + DVE_FIRST + (NG - 1) * DVE_BLOCK)
            last = (NG - 1, NU - 1)
            take_pv(NT)
            take_y(NT, ce)
            scale_y(NT)
            mix(*last, NT, ce)
            divide(NT, NU - 1, ce)
            take_attnT(NG)
            silu(*last, NT, ce)
            for u in range(GT):
                finish(NG - 1, u, (NG - 1) * NU + u + 1, ce, (NG - 1) * (16 * GT // 2) + 16 * (u // 2))

        @block.tensor
        def _(pe):
            te = nc.tensor

            def x_transpose(g):
                pe.wait_ge(xn_ready, g + 1)
                if g:
                    pe.wait_ge(xnT_ready, g)
                for u in range(GT):
                    t = GT * g + u
                    last = te.transpose(psum[:, P * u:P * (u + 1)], xn[:, D * t:D * (t + 1)], ident[:, :])
                last.then_inc(xT_done, 1)

            def qkv(g):
                pe.wait_ge(xnT_ready, g + 1)
                if g:
                    pe.wait_ge(qkv_taken, g)
                for u in range(GT):
                    t = GT * g + u
                    last = te.matmul(bank(1 + u, WCAT), xnT[:, P * t:P * (t + 1)], wcat_sb[:, :], start=True, stop=True)
                last.then_inc(qkv_done, 1)

            def parts_transpose(g):
                pe.wait_ge(lo_ready, g + 1)
                if g:
                    pe.wait_ge(partsT_act, g)
                    pe.wait_ge(partsT_dve, g)
                for s in range(2 * PARTS):
                    qk, part = s // PARTS, s % PARTS
                    for u in range(GT):
                        last = te.transpose(parts_ps[:, s, u, :], split[:, part, u, D * qk:D * (qk + 1)], ident16[:, :])
                last.then_inc(partsT_done, 1)

            pe.wait_ge(ident_ready, 1)
            pe.wait_ge(in_w, 32)
            x_transpose(0)
            qkv(0)
            for g in range(NG):
                if g + 1 < NG:
                    x_transpose(g + 1)
                    qkv(g + 1)
                parts_transpose(g)
            pe.wait_ge(qkv_taken, NG)
            pe.wait_ge(partsT_act, NG)
            pe.wait_ge(partsT_dve, NG)
            pe.wait_ge(in_wb, 64)

            with pe.If(scores_may_be_large(pe)):
                with pe.Fori(0, NG) as i:
                    for u in range(NU):
                        pe.wait_ge(max_operands_in, (i * NU + u + 1) * 16 * 2 * PARTS)
                        for m in range(MAXN):
                            head, q = m // GT, m % GT
                            pe.wait_ge(max_taken, (i * NU + u) * MAXN + m - 1 + CREDIT)
                            for j in range(2):
                                last = te.matmul(bank(2 * (m % 2) + j), q_op[:, 0, head, P * q:P * (q + 1)],
                                                 k_op[:, 0, head, GW * j:GW * (j + 1)], start=True, stop=True)
                            last.then_inc(max_scores_done, 1)
                pe.wait_ge(shift_ready, 1)
                for t in range(NT):
                    last = te.transpose(psum[0:H * PARTS, 0:2 * GW].bitcast(BFF6)[:, P * t:P * (t + 1)],
                                        shift[:, t, :, :].rearrange("p h s -> p (h s)"), ident16[:, :])
                last.then_inc(shiftT_done, 1)
                pe.wait_ge(shift_rows_ready, 1)

            def scores(i, u, t, hp, first):
                k = u * STEPS + 2 * t + hp
                back = next(m for m in range(1, 5) if SBUF_OF[k - m] == SBUF_OF[k])
                if not (first and k < back):
                    pe.wait_ge(probs_ready, i * NU * STEPS + k - back + 1)
                for j in range(2):
                    h = 2 * hp + j
                    last = te.matmul(bank(2 * SBUF_OF[k] + j), k_op[:, u % 2, h, P * t:P * (t + 1)],
                                     q_op[:, u % 2, h, :], start=True, stop=True)
                last.then_inc(scores_done, 1)

            def values(i, u, t, first):
                k = u * STEPS + 2 * t
                pe.wait_ge(probs_ready, i * NU * STEPS + k + 2)
                if t == 0:
                    pe.wait_ge(staged, (i * NU + u) * 2 + 2)
                    if not (first and u == 0):
                        pe.wait_ge(pv_taken, i * NU + u)
                for j in range(HP):
                    last = te.matmul(PV[VW * j:VW * (j + 1), :],
                                     v_op[:, u % 2, t, j, :], probs[:, (k + j // 2) % RING, GW * (j % 2):GW * (j % 2 + 1)],
                                     start=(t == 0), stop=(t == KT - 1))
                last.then_inc(pv_done, 1)

            def mm1(i, u, first):
                n = i * NU + u
                pe.wait_ge(staged, n * 2 + 2)
                if not (first and u == 0):
                    pe.wait_ge(y_taken, n)
                te.matmul(FF, xT_op[:, u % 2, :], w1_sb[:, :], start=True, stop=True).then_inc(mm1_done, 1)

            def pv_transpose(passes):
                pe.wait_ge(pv_taken, passes)
                for q in range(GT):
                    last = te.transpose(FF[:, P * q:P * (q + 1)], pv_sb[:, P * q:P * (q + 1)], ident[:, :])
                last.then_inc(pvT_done, 1)

            def attn_transpose(passes):
                pe.wait_ge(attn_ready, passes)
                for q in range(GT):
                    last = te.transpose(FF[:, P * q:P * (q + 1)], attn[:, q, :], ident[:, :])
                last.then_inc(attnT_done, 1)

            def h_transpose(i, u, first):
                n = i * NU + u
                pe.wait_ge(hr_ready, n + 1)
                if not first:
                    pe.wait_ge(proj_taken, n - NU + 1)
                elif u:
                    pe.wait_ge(attn_ready, n)
                for e in range(NE):
                    last = te.transpose(FF[:, P * e:P * (e + 1)], hr[:, D * e:D * (e + 1)], ident[:, :])
                last.then_inc(hT_done, 1)

            def mm2(done):
                pe.wait_ge(hT_ready, done)
                for e in range(NE):
                    last = te.matmul(FF[:, D * e:D * (e + 1)], hT[:, P * e:P * (e + 1)], w2_sb[:, D * e:D * (e + 1)],
                                     start=True, stop=True)
                last.then_inc(mm2_done, 1)

            def project(u, blocks, free, value):
                pe.wait_ge(attnT_ready, blocks)
                pe.wait_ge(free, value)
                te.matmul(FF[:, 0:D], attnT[:, P * u:P * (u + 1)], wproj_sb[:, :], start=True, stop=True).then_inc(
                    proj_done, 1)

            def one_block(i, first):
                for u in range(NU):
                    n = i * NU + u
                    pe.wait_ge(operands_in[u % 2], i * (96 * NU // 2) + 96 * (u // 2 + 1))
                    for t in range(KT):
                        scores(i, u, t, 0, first)
                        scores(i, u, t, 1, first)
                        if t >= 2:
                            values(i, u, t - 2, first)
                        elif u:
                            values(i, u - 1, KT - 2 + t, first)
                        elif not first:
                            values(i - 1, NU - 1, KT - 2 + t, False)
                        if t == 1 and not (first and u == 0):
                            mm2(n)
                        if t == 2:
                            mm1(i, u, first)
                        if t == 3 and not (first and u == 0):
                            pe.wait_ge(h1_taken, n + 1)
                            pv_transpose(n)
                        if t == 5 and u == 0 and not first:
                            attn_transpose(n)
                        if t == 6 and not first:
                            project(u, i, attn_ready, n)
                        if t == 7:
                            h_transpose(i, u, first)

            one_block(0, True)
            with pe.Fori(1, NG) as i:
                one_block(i, False)
            for t in (KT - 2, KT - 1):
                values(NG - 1, NU - 1, t, False)
            mm2(NT)
            pe.wait_ge(y_taken, NT)
            pv_transpose(NT)
            attn_transpose(NT)
            for u in range(GT):
                project(u, NG, attnT_ready if u == 0 else proj_taken, NG if u == 0 else (NG - 1) * NU + u)


_OUTS = [((B, S, D), "float32")]


def kernel(L0_attn_x, L0_attn_Wqkv, L0_attn_bqkv, L0_attn_Wproj, L0_attn_bproj, L0_attn_qn_w, L0_attn_kn_w,
           L0_ffn_gate_W, L0_ffn_gate_b, L0_ffn_W1, L0_ffn_b1, L0_ffn_g1, L0_ffn_be1, L0_ffn_W2, L0_ffn_b2,
           L0_ffn_g2, L0_ffn_be2):
    import concourse.bacc as bacc
    from concourse.bass_utils import run_bass_kernel_spmd

    def flat(*arrays):
        return np.concatenate([np.asarray(a).reshape(1, -1) for a in arrays], axis=1)

    wide = {
        "x": np.asarray(L0_attn_x),
        "wcat": np.concatenate([np.asarray(L0_attn_Wqkv).T, np.asarray(L0_ffn_gate_W)], axis=1),
        "w1": np.asarray(L0_ffn_W1).transpose(1, 0, 2).reshape(D, NE * D),
        "w2": np.asarray(L0_ffn_W2).transpose(1, 0, 2).reshape(D, NE * D),
        "wproj": np.asarray(L0_attn_Wproj).T,
        "row_a": flat(L0_attn_bqkv, L0_ffn_gate_b, L0_attn_qn_w, L0_attn_kn_w),
        "row_b": flat(L0_ffn_b1, L0_ffn_g1, L0_ffn_be1, L0_ffn_b2, L0_ffn_g2, L0_ffn_be2, L0_attn_bproj),
    }
    nc = bacc.Bacc("TRN2", target_bir_lowering=False, num_devices=1)
    arrays, args = {}, {}
    for name, a in wide.items():
        a = np.ascontiguousarray(a)
        arrays[f"in_{name}"] = a
        args[name] = nc.dram_tensor(f"in_{name}", a.shape, mybir.dt.from_np(a.dtype), kind="ExternalInput").ap()
    shape, dtype = _OUTS[0]
    out = nc.dram_tensor("out_0", shape, mybir.dt.from_np(np.dtype(dtype)), kind="ExternalOutput").ap()
    build(nc, out=out, **args)
    r = run_bass_kernel_spmd(nc, [arrays], core_ids=[0])
    return r.results[0]["out_0"]
```

```python
from contextlib import ExitStack

import numpy as np

import concourse.bass as bass
from concourse import mybir

F32 = mybir.dt.float32
BF16 = mybir.dt.bfloat16
I32 = mybir.dt.int32
ALU = mybir.AluOpType
ACT = mybir.ActivationFunctionType
AX_X = mybir.AxisListType.X

P = 128
B, S, D = 2, 1024, 128
H, HD = 16, 8
NE = 4
TOK = B * S
NT = TOK // P
GT = 4
GW = GT * P
NG = TOK // GW
UT = 2
UW = UT * P
NUNIT = TOK // UW
HP = 4
NU = H // HP
KT = S // P
STEPS = 2 * KT
PARTS = 3
QSLOT = 2 * PARTS - 1
QROWS = QSLOT * HD + PARTS
KROWS = PARTS * HD
PAIR = PARTS * KROWS
LN_LOTS = ((0, 2), (2, 8), (8, 16))
RING = 8
SBUFS = 3
BLOCK_STEPS = NU * STEPS
SBUF_OF = [k % SBUFS for k in range(BLOCK_STEPS - 1)] + [1]
assert BLOCK_STEPS % SBUFS == 1
QKV = 3 * D
WCAT = QKV + NE
VW = 32
LN_EPS = 1e-5
RMS_EPS = 1e-6
SCALE = HD ** -0.5
EXP_SAFE = 64.0


STORES = 3 * 16


class Chain:

    def __init__(self, engine, sem, base):
        self.engine, self.sem, self.base, self.n = engine, sem, base, 0

    def link(self, instruction):
        self.n += 1
        instruction.then_inc(self.sem, 1)
        self.engine.wait_ge(self.sem, self.base + self.n)


DVE_PREP = 37
DVE_FIRST = 31
DVE_BLOCK = 41
POOL_PREP = 5
POOL_BLOCK = 16


def build(nc, x, wcat, w1, w2, wproj, row_a, row_b, out):
    with ExitStack() as ctx:
        def sb(name, shape, dt=F32):
            return ctx.enter_context(nc.sbuf_tensor(name, shape, dt))

        def sem(name):
            return ctx.enter_context(nc.semaphore(name))

        q_parts = nc.dram_tensor("q_parts", (QROWS, H, TOK), BF16).ap()
        k_parts = nc.dram_tensor("k_parts", (KROWS, H, TOK), BF16).ap()

        wcat_sb = sb("wcat_sb", [P, WCAT])
        w1_sb = sb("w1_sb", [P, NE * D])
        w2_sb = sb("w2_sb", [P, NE * D])
        wproj_sb = sb("wproj_sb", [P, D])
        rowa = sb("rowa", [P, WCAT + 2 * HD])
        rowb = sb("rowb", [P, 6 * NE * D + D])
        E = NE * D
        b1, g1, be1, b2, g2, be2 = (rowb[:, j * E:(j + 1) * E] for j in range(6))
        bproj = rowb[:, 6 * E:6 * E + D]
        ident = sb("ident", [P, P])
        ident16 = sb("ident16", [P, P], BF16)
        qkw = sb("qkw", [P, 2 * D])

        x_sb = sb("x_sb", [P, NT * D])
        xn = sb("xn", [P, NT * D])
        xnT = sb("xnT", [P, TOK])
        v_sb = sb("v_sb", [P, NT * D])
        gate = sb("gate", [P, NT * D])
        gsc = sb("gsc", [P, NT, NE])
        wgt = sb("wgt", [P, NT * NE])

        stats = sb("stats", [P, NT, 6])
        mv = sb("mv", [P, NT, 2])
        rstd = sb("rstd", [P, NT])
        qk_b = sb("qk_b", [P, 2, UT, 2 * D])
        qk_w = sb("qk_w", [P, 2, UT, 2 * D])
        qk_sq = sb("qk_sq", [P, 2, UT, 2 * D])
        qk_n = sb("qk_n", [P, 2, UT, 2 * D])
        qk_r = sb("qk_r", [P, 2, UT, 2 * D])
        ssum = sb("ssum", [P, 2, UT * 2 * H])
        split = sb("split", [P, 2, PARTS, UT, 2 * D], BF16)
        splitT = sb("splitT", [P, 2, 2 * PARTS, UW], BF16)
        zero_rows = sb("zero_rows", [PARTS * H, TOK], BF16)
        tri = sb("tri", [P, NE, NE])
        cmp_gt = sb("cmp_gt", [P, NT, NE, NE])
        cmp_eq = sb("cmp_eq", [P, NT, NE, NE])
        rank = sb("rank", [P, NT, NE])
        gmax = sb("gmax", [P, NT])
        gexp = sb("gexp", [P, NT, NE])
        gsum = sb("gsum", [P, NT])

        k_op = sb("k_op", [P, 2, HP, S], BF16)
        q_op = sb("q_op", [P, 2, HP, GW], BF16)
        v_op = sb("v_op", [P, 2, KT, HP, VW])
        probs = sb("probs", [P, RING, 2 * GW])
        pv_sb = sb("pv_sb", [P, GW])
        rden = sb("rden", [P, GT, HP])
        attn = sb("attn", [P, GT, D])
        attnT = sb("attnT", [P, GW])

        xT_op = sb("xT_op", [P, 2, P])
        h1 = sb("h1", [P, E])
        st1 = sb("st1", [P, NE, 6])
        mv1 = sb("mv1", [P, NE, 2])
        ve1 = sb("ve1", [P, NE])
        rs1 = sb("rs1", [P, NE])
        hn = sb("hn", [P, E])
        hr = sb("hr", [P, E])
        hT = sb("hT", [P, E])
        y = sb("y", [P, E])
        st2 = sb("st2", [P, NE, 6])
        mv2 = sb("mv2", [P, NE, 2])
        ve2 = sb("ve2", [P, NE])
        rs2 = sb("rs2", [P, NE])
        rw2 = sb("rw2", [P, NE])
        z = sb("z", [P, E])
        z2 = sb("z2", [P, E])
        zs = sb("zs", [P, 2 * D])
        moe = sb("moe", [P, D])
        moe_t = sb("moe_t", [P, D])
        neg = sb("neg", [P, D])
        eneg = sb("eneg", [P, D])
        den = sb("den", [P, D])
        sig = sb("sig", [P, D])
        s_t = sb("s_t", [P, GW])
        sg = sb("sg", [P, GW])
        o_sb = sb("o_sb", [P, GW])
        wprod = sb("wprod", [1, HD])
        wmax = sb("wmax", [1, 1])
        large = sb("large", [1, 1], I32)
        smax = sb("smax", [P, NT, H])
        smax_r = sb("smax_r", [P, NT, H])
        smax_q = sb("smax_q", [P, NT, H])
        shift = sb("shift", [P, NT, PARTS, H], BF16)

        half = sb("half", [P, NE])

        psum = ctx.enter_context(nc.psum_tensor("psum", [P, 8 * 512], F32))

        def bank(n, w=512):
            return psum[:, 512 * n:512 * n + w]

        in_x = [sem(f"in_x{j}") for j in range(len(LN_LOTS))]
        in_w = sem("in_w")
        in_wb = sem("in_wb")
        ident_ready = sem("ident_ready")
        cleared = sem("cleared")
        dve_links = sem("dve_links")
        pool_links = sem("pool_links")
        dve_waits = sem("dve_waits")
        pool_waits = sem("pool_waits")
        lnvar_ready = sem("lnvar_ready")
        lnstd_ready = sem("lnstd_ready")
        xn_ready = sem("xn_ready")
        xT_done = sem("xT_done")
        xnT_ready = sem("xnT_ready")
        qkv_done = sem("qkv_done")
        qkv_taken = sem("qkv_taken")
        qk_ready = sem("qk_ready")
        sq_ready = sem("sq_ready")
        ms_ready = sem("ms_ready")
        rms_ready = sem("rms_ready")
        qkw_ready = sem("qkw_ready")
        qkn_ready = sem("qkn_ready")
        hi_ready = sem("hi_ready")
        res_ready = sem("res_ready")
        mid_ready = sem("mid_ready")
        lo_ready = sem("lo_ready")
        partsT_done = sem("partsT_done")
        partsT_dve = sem("partsT_dve")
        partsT_act = sem("partsT_act")
        stored = [sem(f"stored{g}") for g in range(2)]
        shift_zeroed = sem("shift_zeroed")
        gdiff_ready = sem("gdiff_ready")
        gexp_ready = sem("gexp_ready")
        wgt_ready = sem("wgt_ready")

        large_ready = sem("large_ready")
        max_operands_in = sem("max_operands_in")
        max_scores_done = sem("max_scores_done")
        max_taken = sem("max_taken")
        max_links = sem("max_links")
        shift_ready = sem("shift_ready")
        shiftT_done = sem("shiftT_done")
        shift_rows_ready = sem("shift_rows_ready")
        shift_stored = sem("shift_stored")

        operands_in = [sem(f"operands_in{j}") for j in range(2)]
        scores_done = sem("scores_done")
        probs_ready = sem("probs_ready")
        pv_done = sem("pv_done")
        staged = sem("staged")
        pv_taken = sem("pv_taken")
        pvT_done = sem("pvT_done")
        attn_ready = sem("attn_ready")
        attnT_done = sem("attnT_done")
        attnT_ready = sem("attnT_ready")
        mm1_done = sem("mm1_done")
        h1_taken = sem("h1_taken")
        mv1_ready = sem("mv1_ready")
        rs1_ready = sem("rs1_ready")
        hn_ready = sem("hn_ready")
        hg_ready = sem("hg_ready")
        hr_ready = sem("hr_ready")
        hT_done = sem("hT_done")
        hT_ready = sem("hT_ready")
        mm2_done = sem("mm2_done")
        y_taken = sem("y_taken")
        mv2_ready = sem("mv2_ready")
        rs2_ready = sem("rs2_ready")
        z_ready = sem("z_ready")
        zg_ready = sem("zg_ready")
        neg_ready = sem("neg_ready")
        eneg_ready = sem("eneg_ready")
        proj_done = sem("proj_done")
        proj_taken = sem("proj_taken")
        out_ready = sem("out_ready")
        out_stored = sem("out_stored")

        x_v = x.rearrange("b (t p) d -> p (b t) d", p=P)
        out_v = out.rearrange("b (t p) d -> p (b t) d", p=P)
        x_3 = x_sb[:, :].rearrange("p (t d) -> p t d", d=D)
        def xT_ps(g):
            return bank(g % 2, UW)

        def qkv_ps(g):
            return psum[:, 512 * (2 + 2 * (g % 2)):512 * (4 + 2 * (g % 2))].rearrange("p (t c) -> p t c", t=UT)

        parts_ps = psum[:, 512 * 6:512 * 8].bitcast(BF16)[:, 0:2 * PARTS * UW].rearrange(
            "p (s t c) -> p s t c", s=2 * PARTS, t=UT)
        PV, FF = bank(6), bank(7)

        MAXN = HP * GT
        CREDIT = 2

        def scores_may_be_large(engine):
            engine.wait_ge(large_ready, 1)
            return engine.value_load(large[0:1, 0:1], min_val=0, max_val=1) > 0

        block = ctx.enter_context(nc.Block())

        @block.sync
        def _(sp):
            def load_x(lot):
                lo, hi = LN_LOTS[lot]
                sp.dma_start(x_3[:, lo:hi, :], x_v[:, lo:hi, :]).then_inc(in_x[lot], 16)

            load_x(0)
            sp.dma_start(wcat_sb[:, :], wcat).then_inc(in_w, 16)
            load_x(1)
            sp.dma_start(rowa[:, :], row_a.broadcast_to([P, WCAT + 2 * HD])).then_inc(in_w, 16)
            load_x(2)
            sp.dma_start(w1_sb[:, :], w1).then_inc(in_wb, 16)
            sp.dma_start(w2_sb[:, :], w2).then_inc(in_wb, 16)
            sp.dma_start(wproj_sb[:, :], wproj).then_inc(in_wb, 16)
            sp.dma_start(rowb[:, :], row_b.broadcast_to([P, 6 * E + D])).then_inc(in_wb, 16)
            sp.wait_ge(cleared, 1)
            sp.dma_start(q_parts[QSLOT * HD:, :, :], zero_rows[:, :]).then_inc(shift_zeroed, 16)
            for g in range(NUNIT):
                cols = slice(UW * g, UW * (g + 1))
                sp.wait_ge(partsT_dve, g + 1)
                sp.wait_ge(partsT_act, g + 1)
                for lo, n in ((0, PARTS), (PARTS, QSLOT - PARTS)):
                    sp.dma_start(q_parts[lo * HD:(lo + n) * HD, :, cols].rearrange("(s d) h t -> (d h) s t", d=HD),
                                 splitT[:, g % 2, 0:n, :]).then_inc(stored[g % 2], 16)
                sp.dma_start(k_parts[:, :, cols].rearrange("(s d) h t -> (d h) s t", d=HD),
                             splitT[:, g % 2, PARTS:2 * PARTS, :]).then_inc(stored[g % 2], 16)

            def operand_dmas(i, u, par, arrived):
                for a in range(PARTS):
                    sp.dma_start(k_op[KROWS * a:KROWS * (a + 1), par, :, :],
                                 k_parts[:, HP * u:HP * (u + 1), bass.ds((i // 2) * S, S)]).then_inc(arrived, 16)
                    rows = KROWS + (PARTS if a == PARTS - 1 else 0)
                    sp.dma_start(q_op[KROWS * a:KROWS * a + rows, par, :, :],
                                 q_parts[HD * a:HD * a + rows, HP * u:HP * (u + 1), bass.ds(i * GW, GW)]).then_inc(arrived, 16)

            def load_operands(i, u, first):
                par = u % 2
                if not (first and u < 2):
                    sp.wait_ge(scores_done, i * NU * STEPS + STEPS * (u - 1))
                operand_dmas(i, u, par, operands_in[par])

            def store_block(i, count):
                sp.wait_ge(out_ready, count)
                sp.dma_start(out_v[:, bass.ds(i * GT, GT), :], o_sb[:, :].rearrange("p (t d) -> p t d", d=D)).then_inc(
                    out_stored, 16)

            for par in range(2):
                sp.wait_ge(stored[par], STORES * NUNIT // 2)
            sp.wait_ge(shift_zeroed, 16)
            sp.wait_ge(cleared, 3)
            with sp.If(scores_may_be_large(sp)):
                with sp.Fori(0, NG) as i:
                    for u in range(NU):
                        sp.wait_ge(max_taken, (i * NU + u) * MAXN + CREDIT)
                        operand_dmas(i, u, 0, max_operands_in)
                sp.wait_ge(shift_rows_ready, 1)
                sp.dma_start(q_parts[QSLOT * HD:, :, :], zero_rows[:, :]).then_inc(shift_stored, 16)
                sp.wait_ge(shift_stored, 16)
            for u in range(NU):
                load_operands(0, u, True)
            for u in range(NU):
                load_operands(1, u, False)
            with sp.Fori(2, NG) as i:
                for u in range(NU):
                    load_operands(i, u, False)
                    if u == 0:
                        store_block(i - 2, i - 1)
            store_block(NG - 2, NG - 1)
            store_block(NG - 1, NG)
            sp.wait_ge(out_stored, 16 * NG)

        @block.gpsimd
        def _(pool):
            gp = nc.gpsimd
            ch = Chain(pool, pool_links, 0)
            ch.link(gp.memset(ident[:], 0.0))
            ch.link(gp.affine_select(out=ident[:, :], in_=ident[:, :], compare_op=ALU.not_equal, fill=1.0,
                                     base=0, pattern=[[-1, P]], channel_multiplier=1))
            gp.tensor_copy(ident16[:, :], ident[:, :]).then_inc(ident_ready, 1)
            gp.memset(zero_rows[:], 0.0).then_inc(cleared, 1)
            pool.wait_ge(cleared, 1)
            gp.memset(q_op[:], 0.0).then_inc(cleared, 1)
            pool.wait_ge(cleared, 2)
            gp.memset(k_op[:], 1.0).then_inc(cleared, 1)
            gp.memset(half[:], -0.5)
            ch.link(gp.memset(v_op[:], 0.0))
            ch.link(gp.memset(v_op[:, :, :, :, HD:HD + 1], 1.0))
            pool.wait_ge(in_w, 32)
            qn = rowa[:, WCAT:WCAT + HD]
            kn = rowa[:, WCAT + HD:WCAT + 2 * HD]
            gp.tensor_scalar(qkw[:, 0:D].rearrange("p (h d) -> p h d", d=HD),
                             qn.unsqueeze(1).broadcast_to([P, H, HD]), SCALE, 1.0, ALU.mult, ALU.mult)
            ch.link(gp.tensor_scalar(qkw[:, D:2 * D].rearrange("p (h d) -> p h d", d=HD),
                                     kn.unsqueeze(1).broadcast_to([P, H, HD]), 1.0, 1.0, ALU.mult, ALU.mult))
            for g in range(NUNIT):
                pool.wait_ge(qk_ready, g + 1)
                if g >= 2:
                    pool.wait_ge(qkn_ready, g - 1)
                gp.tensor_tensor(qk_w[:, g % 2, :, :], qk_b[:, g % 2, :, :],
                                 qkw[:, :].unsqueeze(1).broadcast_to([P, UT, 2 * D]), ALU.mult).then_inc(qkw_ready, 1)
            assert ch.n == POOL_PREP, ("POOL_PREP", ch.n)

            def stage(i, u):
                pool.sem_inc(pool_waits, 1)
                v_b = v_sb[:, bass.ds((i // 2) * (KT * D), KT * D)].rearrange("p (t c) -> p t c", c=D)
                gp.tensor_copy(v_op[:, u % 2, :, :, 0:HD],
                               v_b[:, :, HP * HD * u:HP * HD * (u + 1)].rearrange("p t (h d) -> p t h d", d=HD)
                               ).then_inc(staged, 1)
                gp.tensor_copy(xT_op[:, u % 2, :], xnT[:, bass.ds(i * GW + u * P, P)]).then_inc(staged, 1)

            def power(ch, dst, tmp, mv_):
                pool.sem_inc(pool_waits, 1)
                ch.link(gp.tensor_scalar(tmp[:, :], mv_[:, :, 1], LN_EPS, 1.0, ALU.add, ALU.mult))
                return gp.tensor_tensor(dst[:, :], tmp[:, :], half[:, :], ALU.pow)

            def experts_b(i, u, ch, prev):
                pool.wait_ge(mv2_ready, prev)
                ch.link(power(ch, rs2, ve2, mv2))
                gp.tensor_tensor(rw2[:, :], rs2[:, :], wgt[:, bass.ds((i * NU + u) * NE, NE)],
                                 ALU.mult).then_inc(rs2_ready, 1)

            def scale_b(prev):
                pool.wait_ge(z_ready, prev)
                gp.tensor_tensor(z2[:, :], z[:, :], g2, ALU.mult).then_inc(zg_ready, 1)

            def one_block(i, ch, first):
                for u in range(NU):
                    n = i * NU + u
                    if not (first and u == 0):
                        experts_b(i if u else i - 1, (u - 1) % NU, ch, n)
                    if not (first and u == 0):
                        pool.wait_ge(pv_done, i * NU * KT + KT * u)
                    stage(i if u < NU - 1 else i + 1, (u + 1) % NU)
                    pool.wait_ge(mv1_ready, n + 1)
                    power(ch, rs1, ve1, mv1).then_inc(rs1_ready, 1)
                    if not (first and u == 0):
                        scale_b(n)
                    pool.wait_ge(hn_ready, n + 1)
                    ch.link(gp.tensor_tensor(hn[:, :], hn[:, :], g1, ALU.mult))
                    gp.tensor_tensor(hn[:, :], hn[:, :], be1, ALU.add).then_inc(hg_ready, 1)

            pool.wait_ge(qkv_taken, NUNIT)
            pool.wait_ge(xnT_ready, NUNIT)
            stage(0, 0)
            pool.wait_ge(in_wb, 64)
            pool.wait_ge(wgt_ready, 1)
            c0 = Chain(pool, pool_links, POOL_PREP)
            one_block(0, c0, True)
            assert c0.n == POOL_BLOCK - 2, ("POOL_BLOCK", c0.n + 2)
            with pool.Fori(1, NG - 1) as i:
                ci = Chain(pool, pool_links, (i - 1) * POOL_BLOCK + (POOL_PREP + POOL_BLOCK - 2))
                one_block(i, ci, False)
                assert ci.n == POOL_BLOCK, ("POOL_BLOCK", ci.n)
            cl = Chain(pool, pool_links, POOL_PREP + (NG - 1) * POOL_BLOCK - 2)
            last = NG - 1
            for u in range(NU):
                n = last * NU + u
                experts_b(last if u else last - 1, (u - 1) % NU, cl, n)
                if u < NU - 1:
                    pool.wait_ge(pv_done, last * NU * KT + KT * u)
                    stage(last, u + 1)
                pool.wait_ge(mv1_ready, n + 1)
                power(cl, rs1, ve1, mv1).then_inc(rs1_ready, 1)
                scale_b(n)
                pool.wait_ge(hn_ready, n + 1)
                cl.link(gp.tensor_tensor(hn[:, :], hn[:, :], g1, ALU.mult))
                gp.tensor_tensor(hn[:, :], hn[:, :], be1, ALU.add).then_inc(hg_ready, 1)
            experts_b(last, NU - 1, cl, NT)
            scale_b(NT)

        @block.scalar
        def _(act):
            sc = nc.scalar

            def ln_std(lot):
                lo, hi = LN_LOTS[lot]
                act.wait_ge(lnvar_ready, lot + 1)
                sc.activation(rstd[:, lo:hi], rstd[:, lo:hi], ACT.Sqrt).then_inc(lnstd_ready, 1)

            def copy_xT(g):
                act.wait_ge(xT_done, g + 1)
                sc.activation(xnT[:, UW * g:UW * (g + 1)], xT_ps(g), ACT.Copy).then_inc(xnT_ready, 1)

            def mid_part(g):
                act.wait_ge(res_ready, g + 1)
                sc.activation(split[:, g % 2, 1, :, :], qk_r[:, g % 2, :, :], ACT.Copy).then_inc(mid_ready, 1)

            def copy_parts(g):
                act.wait_ge(partsT_done, g + 1)
                if g >= 2:
                    act.wait_ge(stored[g % 2], STORES * (g // 2))
                sc.activation(splitT[:, g % 2, 4:6, :], parts_ps[:, 4:6, :, :], ACT.Copy).then_inc(partsT_act, 1)

            ln_std(0)
            copy_xT(0)
            ln_std(1)
            copy_xT(1)
            for g in range(NUNIT + 1):
                if g < NUNIT:
                    act.wait_ge(qk_ready, g + 1)
                    sc.activation(qk_sq[:, g % 2, :, :], qk_b[:, g % 2, :, :], ACT.Square).then_inc(sq_ready, 1)
                if g:
                    mid_part(g - 1)
                if g < NUNIT:
                    act.wait_ge(ms_ready, g + 1)
                    sc.activation(ssum[:, g % 2, :], ssum[:, g % 2, :], ACT.Sqrt).then_inc(rms_ready, 1)
                if g == 1:
                    ln_std(2)
                if g + 2 < NUNIT:
                    copy_xT(g + 2)
                if g < NUNIT:
                    act.wait_ge(qkn_ready, g + 1)
                    if g >= 2:
                        act.wait_ge(partsT_done, g - 1)
                    sc.activation(split[:, g % 2, 0, :, :], qk_n[:, g % 2, :, :], ACT.Copy).then_inc(hi_ready, 1)
                if g:
                    copy_parts(g - 1)
            act.wait_ge(gdiff_ready, 1)
            sc.activation(gexp[:, :, :], gexp[:, :, :], ACT.Exp).then_inc(gexp_ready, 1)

            def exp_step(i, k, first):
                n = i * NU * STEPS + k
                act.wait_ge(scores_done, n + 1)
                if not (first and k < RING):
                    act.wait_ge(pv_done, i * NU * KT + (k - RING) // 2 + 1)
                sc.activation(probs[:, k % RING, :], bank(2 * SBUF_OF[k], 2 * GW),
                              ACT.Exp).then_inc(probs_ready, 1)

            def exp_neg(count):
                act.wait_ge(neg_ready, count)
                sc.activation(eneg[:, :], neg[:, :], ACT.Exp).then_inc(eneg_ready, 1)

            def one_block(i, first):
                for u in range(NU):
                    for k in range(STEPS):
                        exp_step(i, u * STEPS + k, first)
                        if k == STEPS - 2 and not (first and u == 0):
                            exp_neg(i * NU + u)

            one_block(0, True)
            with act.Fori(1, NG) as i:
                one_block(i, False)
            exp_neg(NT)

        @block.vector
        def _(dve):
            ve = nc.vector
            ch = Chain(dve, dve_links, 0)

            def ln_stats(lot):
                lo, hi = LN_LOTS[lot]
                dve.wait_ge(in_x[lot], 16)
                for t in range(lo, hi):
                    st = ve.bn_stats(stats[:, t, :], x_3[:, t, :])
                ch.link(st)
                for t in range(lo, hi):
                    st = ve.bn_aggr(mv[:, t, :], stats[:, t, :])
                ch.link(st)
                ve.tensor_scalar(rstd[:, lo:hi], mv[:, lo:hi, 1], LN_EPS, None, ALU.add).then_inc(lnvar_ready, 1)

            def ln_recip(lot):
                lo, hi = LN_LOTS[lot]
                dve.wait_ge(lnstd_ready, lot + 1)
                ch.link(ve.reciprocal(rstd[:, lo:hi], rstd[:, lo:hi]))

            def ln_apply(g):
                for t in range(UT * g, UT * (g + 1)):
                    last = ve.tensor_scalar(xn[:, D * t:D * (t + 1)], x_sb[:, D * t:D * (t + 1)], mv[:, t, 0:1],
                                            rstd[:, t:t + 1], ALU.subtract, ALU.mult)
                last.then_inc(xn_ready, 1)

            bias = rowa[:, 0:WCAT]
            for e in range(1, NE):
                ve.memset(tri[:, e, 0:e], 1.0)
            for e in range(NE):
                st = ve.memset(tri[:, e, e:NE], 0.0)
            ch.link(st)
            ln_stats(0)
            ln_recip(0)
            ln_apply(0)
            ln_stats(1)
            ln_recip(1)
            ln_apply(1)
            dve.wait_ge(in_w, 32)
            ch.link(ve.tensor_tensor(wprod[:, :], rowa[0:1, WCAT:WCAT + HD], rowa[0:1, WCAT + HD:WCAT + 2 * HD],
                                     ALU.mult))
            ch.link(ve.tensor_tensor(wprod[:, :], wprod[:, :], wprod[:, :], ALU.mult))
            ch.link(ve.tensor_reduce(wmax[:, :], wprod[:, :], AX_X, ALU.max))
            ve.tensor_scalar(large[:, :], wmax[:, :], (EXP_SAFE / (SCALE * HD)) ** 2, None,
                             ALU.is_gt).then_inc(large_ready, 1)
            def take_qkv(g):
                dve.wait_ge(qkv_done, g + 1)
                if g >= 2:
                    dve.wait_ge(qkw_ready, g - 1)
                    dve.wait_ge(sq_ready, g - 1)
                ve.tensor_tensor(qk_b[:, g % 2, :, :], qkv_ps(g)[:, :, 0:2 * D],
                                 bias[:, 0:2 * D].unsqueeze(1).broadcast_to([P, UT, 2 * D]),
                                 ALU.add).then_inc(qk_ready, 1)
                ve.tensor_tensor(v_sb[:, UW * g:UW * (g + 1)].rearrange("p (t c) -> p t c", t=UT),
                                 qkv_ps(g)[:, :, 2 * D:QKV],
                                 bias[:, 2 * D:QKV].unsqueeze(1).broadcast_to([P, UT, D]), ALU.add)
                ve.tensor_tensor(gsc[:, UT * g:UT * (g + 1), :], qkv_ps(g)[:, :, QKV:WCAT],
                                 bias[:, QKV:WCAT].unsqueeze(1).broadcast_to([P, UT, NE]),
                                 ALU.add).then_inc(qkv_taken, 1)

            def mean_square(g):
                dve.wait_ge(sq_ready, g + 1)
                ch.link(ve.tensor_reduce(ssum[:, g % 2, :],
                                         qk_sq[:, g % 2, :, :].rearrange("p t (h d) -> p (t h) d", d=HD),
                                         AX_X, ALU.add))
                ve.tensor_scalar(ssum[:, g % 2, :], ssum[:, g % 2, :], 1.0 / HD, RMS_EPS,
                                 ALU.mult, ALU.add).then_inc(ms_ready, 1)

            def rms_apply(g):
                dve.wait_ge(rms_ready, g + 1)
                ch.link(ve.reciprocal(ssum[:, g % 2, :], ssum[:, g % 2, :]))
                dve.wait_ge(qkw_ready, g + 1)
                for x in range(2):
                    last = ve.tensor_tensor(
                        qk_n[:, g % 2, :, D * x:D * (x + 1)].rearrange("p t (d h) -> p t h d", d=HD),
                        qk_w[:, g % 2, :, D * x:D * (x + 1)].rearrange("p t (h d) -> p t h d", d=HD),
                        ssum[:, g % 2, :].rearrange("p (t y) -> p t y", t=UT)[:, :, H * x:H * (x + 1)].unsqueeze(3)
                        .broadcast_to([P, UT, H, HD]), ALU.mult)
                last.then_inc(qkn_ready, 1)

            def residue(g):
                dve.wait_ge(hi_ready, g + 1)
                ve.tensor_tensor(qk_r[:, g % 2, :, :], qk_n[:, g % 2, :, :], split[:, g % 2, 0, :, :],
                                 ALU.subtract).then_inc(res_ready, 1)

            def lo_part(g):
                dve.wait_ge(mid_ready, g + 1)
                ve.tensor_tensor(split[:, g % 2, 2, :, :], qk_r[:, g % 2, :, :], split[:, g % 2, 1, :, :],
                                 ALU.subtract).then_inc(lo_ready, 1)

            def copy_parts(g):
                dve.wait_ge(partsT_done, g + 1)
                if g >= 2:
                    dve.wait_ge(stored[g % 2], STORES * (g // 2))
                ve.tensor_copy(splitT[:, g % 2, 0:4, :], parts_ps[:, 0:4, :, :]).then_inc(partsT_dve, 1)

            for g in range(NUNIT + 1):
                if g < NUNIT:
                    take_qkv(g)
                if g:
                    residue(g - 1)
                if g < NUNIT:
                    mean_square(g)
                if g:
                    lo_part(g - 1)
                if g == 1:
                    ln_stats(2)
                    ln_recip(2)
                if g + 2 < NUNIT:
                    ln_apply(g + 2)
                if g < NUNIT:
                    rms_apply(g)
                if g:
                    copy_parts(g - 1)

            of_f = gsc[:, :, :].unsqueeze(2).broadcast_to([P, NT, NE, NE])
            of_e = gsc[:, :, :].unsqueeze(3).broadcast_to([P, NT, NE, NE])
            flat = "p t e f -> p t (e f)"
            dve.wait_ge(qkv_taken, NUNIT)
            ve.tensor_reduce(gmax[:, :], gsc[:, :, :], AX_X, ALU.max)
            ve.tensor_tensor(cmp_gt[:, :, :, :], of_f, of_e, ALU.is_gt)
            ch.link(ve.tensor_tensor(cmp_eq[:, :, :, :], of_f, of_e, ALU.is_equal))
            ve.tensor_tensor(gexp[:, :, :], gsc[:, :, :], gmax[:, :].unsqueeze(2).broadcast_to([P, NT, NE]),
                             ALU.subtract).then_inc(gdiff_ready, 1)
            ch.link(ve.tensor_tensor(cmp_eq[:, :, :, :].rearrange(flat), cmp_eq[:, :, :, :].rearrange(flat),
                                     tri[:, :, :].rearrange("p e f -> p (e f)").unsqueeze(1)
                                     .broadcast_to([P, NT, NE * NE]), ALU.mult))
            ch.link(ve.tensor_tensor(cmp_gt[:, :, :, :], cmp_gt[:, :, :, :], cmp_eq[:, :, :, :], ALU.add))
            ch.link(ve.tensor_reduce(rank[:, :, :], cmp_gt[:, :, :, :], AX_X, ALU.add))
            ch.link(ve.tensor_scalar(rank[:, :, :], rank[:, :, :], 1.5, None, ALU.is_lt))
            dve.wait_ge(gexp_ready, 1)
            ch.link(ve.tensor_tensor(gexp[:, :, :], gexp[:, :, :], rank[:, :, :], ALU.mult))
            ch.link(ve.tensor_reduce(gsum[:, :], gexp[:, :, :], AX_X, ALU.add))
            ch.link(ve.reciprocal(gsum[:, :], gsum[:, :]))
            ve.tensor_tensor(wgt[:, :].rearrange("p (t e) -> p t e", e=NE), gexp[:, :, :],
                             gsum[:, :].unsqueeze(2).broadcast_to([P, NT, NE]), ALU.mult).then_inc(wgt_ready, 1)
            dve.wait_ge(wgt_ready, 1)
            dve.wait_ge(in_wb, 64)
            assert ch.n == DVE_PREP, ("DVE_PREP", ch.n)

            with dve.If(scores_may_be_large(dve)):
                dve.sem_inc(max_taken, CREDIT)
                with dve.Fori(0, NG) as i:
                    for u in range(NU):
                        for m in range(MAXN):
                            head, q = HP * u + m // GT, m % GT
                            dve.wait_ge(max_scores_done, (i * NU + u) * MAXN + m + 1)
                            dve.sem_inc(dve_waits, 1)
                            ve.tensor_reduce(smax[:, bass.ds(i * GT + q, 1), head], bank(2 * (m % 2), 2 * GW),
                                             AX_X, ALU.max).then_inc(max_taken, 1)
                dve.wait_ge(max_taken, NG * NU * MAXN + CREDIT)
                cm = Chain(dve, max_links, 0)
                cm.link(ve.tensor_scalar(smax_r[:, :, :], smax[:, :, :], -1.0, None, ALU.mult))
                cm.link(ve.tensor_copy(shift[:, :, 0, :], smax_r[:, :, :]))
                cm.link(ve.tensor_tensor(smax_q[:, :, :], smax_r[:, :, :], shift[:, :, 0, :], ALU.subtract))
                cm.link(ve.tensor_copy(shift[:, :, 1, :], smax_q[:, :, :]))
                ve.tensor_tensor(shift[:, :, 2, :], smax_q[:, :, :], shift[:, :, 1, :],
                                 ALU.subtract).then_inc(shift_ready, 1)
                dve.wait_ge(shiftT_done, 1)
                dve.wait_ge(shift_zeroed, 16)
                ve.tensor_copy(zero_rows[:, :], psum[0:H * PARTS, 0:2 * GW].bitcast(BF16)).then_inc(shift_rows_ready, 1)

            def col(e):
                return slice(D * e, D * (e + 1))

            def take_y(n_done, ch):
                dve.wait_ge(mm2_done, n_done)
                ve.tensor_tensor(y[:, :], FF, b2, ALU.add).then_inc(y_taken, 1)
                dve.wait_ge(y_taken, n_done)
                for e in range(NE):
                    st = ve.bn_stats(st2[:, e, :], y[:, col(e)])
                ch.link(st)
                dve.sem_inc(dve_waits, 1)
                for e in range(NE):
                    st = ve.bn_aggr(mv2[:, e, :], st2[:, e, :])
                st.then_inc(mv2_ready, 1)

            def take_h(n_done, ch):
                dve.wait_ge(mm1_done, n_done)
                ve.tensor_tensor(h1[:, :], FF, b1, ALU.add).then_inc(h1_taken, 1)
                dve.wait_ge(h1_taken, n_done)
                for e in range(NE):
                    st = ve.bn_stats(st1[:, e, :], h1[:, col(e)])
                ch.link(st)
                dve.sem_inc(dve_waits, 1)
                for e in range(NE):
                    st = ve.bn_aggr(mv1[:, e, :], st1[:, e, :])
                st.then_inc(mv1_ready, 1)

            def normalize(dst, src, mv_, rs, done):
                for e in range(NE):
                    st = ve.tensor_scalar(dst[:, col(e)], src[:, col(e)], mv_[:, e, 0:1], rs[:, e:e + 1],
                                          ALU.subtract, ALU.mult)
                st.then_inc(done, 1)

            def scale_y(n_done):
                dve.wait_ge(rs2_ready, n_done)
                normalize(z, y, mv2, rw2, z_ready)

            def mix(i, u, n_done, ch):
                t = i * NU + u
                dve.wait_ge(zg_ready, n_done)
                for e in range(NE):
                    st = ve.scalar_tensor_tensor(z[:, col(e)], be2[:, col(e)], wgt[:, bass.ds(t * NE + e, 1)],
                                                 z2[:, col(e)], ALU.mult, ALU.add)
                ch.link(st)
                ch.link(ve.tensor_tensor(zs[:, :], z[:, 0:2 * D], z[:, 2 * D:4 * D], ALU.add))
                ch.link(ve.tensor_tensor(moe_t[:, :], zs[:, 0:D], zs[:, D:2 * D], ALU.add))
                ch.link(ve.tensor_tensor(moe[:, :], moe_t[:, :], xn[:, bass.ds(t * D, D)], ALU.add))
                ve.tensor_scalar(neg[:, :], moe[:, :], -1.0, 87.0, ALU.mult, ALU.min).then_inc(neg_ready, 1)

            def silu(i, u, n_done, ch):
                dve.wait_ge(eneg_ready, n_done)
                ch.link(ve.tensor_scalar(den[:, :], eneg[:, :], 1.0, None, ALU.add))
                ch.link(ve.reciprocal(sig[:, :], den[:, :]))
                ch.link(ve.tensor_tensor(gate[:, bass.ds((i * NU + u) * D, D)], moe[:, :], sig[:, :], ALU.mult))

            def take_pv(passes):
                dve.wait_ge(pv_done, KT * passes)
                ve.tensor_copy(pv_sb[:, :], PV).then_inc(pv_taken, 1)

            def divide(passes, u, ch):
                dve.wait_ge(pvT_done, passes)
                pvT = FF.rearrange("p (q h c) -> p q h c", q=GT, h=HP)
                ch.link(ve.reciprocal(rden[:, :, :], pvT[:, :, :, HD]))
                ve.tensor_tensor(attn[:, :, HP * HD * u:HP * HD * (u + 1)].rearrange("p q (h d) -> p q h d", d=HD),
                                 pvT[:, :, :, 0:HD], rden[:, :, :].unsqueeze(3).broadcast_to([P, GT, HP, HD]),
                                 ALU.mult).then_inc(attn_ready, 1)

            def take_attnT(blocks):
                dve.wait_ge(attnT_done, blocks)
                ve.tensor_copy(attnT[:, :], FF).then_inc(attnT_ready, 1)

            def relu(n_done):
                dve.wait_ge(hg_ready, n_done)
                ve.tensor_scalar(hr[:, :], hn[:, :], 0.0, None, ALU.max).then_inc(hr_ready, 1)

            def take_hT(n_done):
                dve.wait_ge(hT_done, n_done)
                ve.tensor_copy(hT[:, :], FF).then_inc(hT_ready, 1)

            def finish(i, blocks, ch, stored_before):
                cols = bass.ds(i * GW, GW)
                dve.wait_ge(proj_done, blocks)
                ve.tensor_tensor(s_t[:, :].rearrange("p (t d) -> p t d", d=D), FF.rearrange("p (t d) -> p t d", d=D),
                                 bproj.unsqueeze(1).broadcast_to([P, GT, D]), ALU.add).then_inc(proj_taken, 1)
                dve.wait_ge(proj_taken, blocks)
                ch.link(ve.tensor_tensor(sg[:, :], s_t[:, :], gate[:, cols], ALU.mult))
                if stored_before:
                    dve.wait_ge(out_stored, (blocks - 1) * 16)
                ve.tensor_tensor(o_sb[:, :], sg[:, :], x_sb[:, cols], ALU.add).then_inc(out_ready, 1)

            def one_block(i, ch, first, second):
                for u in range(NU):
                    n = i * NU + u
                    head = first and u == 0
                    before = (i if u else i - 1, (u - 1) % NU)
                    if not head:
                        take_pv(n)
                        take_y(n, ch)
                    take_h(n + 1, ch)
                    if not head:
                        scale_y(n)
                    dve.wait_ge(rs1_ready, n + 1)
                    normalize(hn, h1, mv1, rs1, hn_ready)
                    if not head:
                        divide(n, (u - 1) % NU, ch)
                        mix(*before, n, ch)
                    if u == 0 and not first:
                        take_attnT(i)
                    relu(n + 1)
                    if u == 1 and not first:
                        finish(i - 1, i, ch, not second)
                    take_hT(n + 1)
                    if not head:
                        silu(*before, n, ch)

            c0 = Chain(dve, dve_links, DVE_PREP)
            one_block(0, c0, True, False)
            assert c0.n == DVE_FIRST, ("DVE_FIRST", c0.n)
            c1 = Chain(dve, dve_links, DVE_PREP + DVE_FIRST)
            one_block(1, c1, False, True)
            assert c1.n == DVE_BLOCK, ("DVE_BLOCK", c1.n)
            with dve.Fori(2, NG) as i:
                ci = Chain(dve, dve_links, (i - 2) * DVE_BLOCK + (DVE_PREP + DVE_FIRST + DVE_BLOCK))
                one_block(i, ci, False, False)
            ce = Chain(dve, dve_links, DVE_PREP + DVE_FIRST + (NG - 1) * DVE_BLOCK)
            last = (NG - 1, NU - 1)
            take_pv(NT)
            take_y(NT, ce)
            scale_y(NT)
            mix(*last, NT, ce)
            divide(NT, NU - 1, ce)
            take_attnT(NG)
            silu(*last, NT, ce)
            finish(NG - 1, NG, ce, True)

        @block.tensor
        def _(pe):
            te = nc.tensor

            def x_transpose(g):
                pe.wait_ge(xn_ready, g + 1)
                if g >= 2:
                    pe.wait_ge(xnT_ready, g - 1)
                for u in range(UT):
                    t = UT * g + u
                    last = te.transpose(xT_ps(g)[:, P * u:P * (u + 1)], xn[:, D * t:D * (t + 1)], ident[:, :])
                last.then_inc(xT_done, 1)

            def qkv(g):
                pe.wait_ge(xnT_ready, g + 1)
                if g >= 2:
                    pe.wait_ge(qkv_taken, g - 1)
                for u in range(UT):
                    t = UT * g + u
                    last = te.matmul(qkv_ps(g)[:, u, 0:WCAT], xnT[:, P * t:P * (t + 1)], wcat_sb[:, :],
                                     start=True, stop=True)
                last.then_inc(qkv_done, 1)

            def parts_transpose(g):
                pe.wait_ge(lo_ready, g + 1)
                if g:
                    pe.wait_ge(partsT_act, g)
                    pe.wait_ge(partsT_dve, g)
                for s in range(2 * PARTS):
                    qk, part = s // PARTS, s % PARTS
                    for u in range(UT):
                        last = te.transpose(parts_ps[:, s, u, :], split[:, g % 2, part, u, D * qk:D * (qk + 1)],
                                            ident16[:, :])
                last.then_inc(partsT_done, 1)

            pe.wait_ge(ident_ready, 1)
            x_transpose(0)
            pe.wait_ge(in_w, 32)
            qkv(0)
            x_transpose(1)
            qkv(1)
            for g in range(NUNIT):
                if g + 2 < NUNIT:
                    x_transpose(g + 2)
                    qkv(g + 2)
                parts_transpose(g)
            pe.wait_ge(qkv_taken, NUNIT)
            pe.wait_ge(partsT_act, NUNIT)
            pe.wait_ge(partsT_dve, NUNIT)
            pe.wait_ge(in_wb, 64)

            with pe.If(scores_may_be_large(pe)):
                with pe.Fori(0, NG) as i:
                    for u in range(NU):
                        pe.wait_ge(max_operands_in, (i * NU + u + 1) * 16 * 2 * PARTS)
                        for m in range(MAXN):
                            head, q = m // GT, m % GT
                            pe.wait_ge(max_taken, (i * NU + u) * MAXN + m - 1 + CREDIT)
                            for j in range(2):
                                last = te.matmul(bank(2 * (m % 2) + j), q_op[:, 0, head, P * q:P * (q + 1)],
                                                 k_op[:, 0, head, GW * j:GW * (j + 1)], start=True, stop=True)
                            last.then_inc(max_scores_done, 1)
                pe.wait_ge(shift_ready, 1)
                for t in range(NT):
                    last = te.transpose(psum[0:H * PARTS, 0:2 * GW].bitcast(BF16)[:, P * t:P * (t + 1)],
                                        shift[:, t, :, :].rearrange("p s h -> p (s h)"), ident16[:, :])
                last.then_inc(shiftT_done, 1)
                pe.wait_ge(shift_rows_ready, 1)

            def scores(i, u, t, hp, first):
                k = u * STEPS + 2 * t + hp
                back = next(m for m in range(1, 5) if SBUF_OF[k - m] == SBUF_OF[k])
                if not (first and k < back):
                    pe.wait_ge(probs_ready, i * NU * STEPS + k - back + 1)
                for j in range(2):
                    h = 2 * hp + j
                    last = te.matmul(bank(2 * SBUF_OF[k] + j), k_op[:, u % 2, h, P * t:P * (t + 1)],
                                     q_op[:, u % 2, h, :], start=True, stop=True)
                last.then_inc(scores_done, 1)

            def values(i, u, t, first):
                k = u * STEPS + 2 * t
                pe.wait_ge(probs_ready, i * NU * STEPS + k + 2)
                if t == 0:
                    pe.wait_ge(staged, (i * NU + u) * 2 + 2)
                    if not (first and u == 0):
                        pe.wait_ge(pv_taken, i * NU + u)
                for j in range(HP):
                    last = te.matmul(PV[VW * j:VW * (j + 1), :],
                                     v_op[:, u % 2, t, j, :], probs[:, (k + j // 2) % RING, GW * (j % 2):GW * (j % 2 + 1)],
                                     start=(t == 0), stop=(t == KT - 1))
                last.then_inc(pv_done, 1)

            def mm1(i, u, first):
                n = i * NU + u
                pe.wait_ge(staged, n * 2 + 2)
                if not (first and u == 0):
                    pe.wait_ge(y_taken, n)
                te.matmul(FF, xT_op[:, u % 2, :], w1_sb[:, :], start=True, stop=True).then_inc(mm1_done, 1)

            def pv_transpose(passes):
                pe.wait_ge(pv_taken, passes)
                for q in range(GT):
                    last = te.transpose(FF[:, P * q:P * (q + 1)], pv_sb[:, P * q:P * (q + 1)], ident[:, :])
                last.then_inc(pvT_done, 1)

            def attn_transpose(passes):
                pe.wait_ge(attn_ready, passes)
                for q in range(GT):
                    last = te.transpose(FF[:, P * q:P * (q + 1)], attn[:, q, :], ident[:, :])
                last.then_inc(attnT_done, 1)

            def h_transpose(i, u, first):
                n = i * NU + u
                pe.wait_ge(hr_ready, n + 1)
                if u == 0 and not first:
                    pe.wait_ge(attnT_ready, i)
                elif u == 1 and not first:
                    pe.wait_ge(proj_taken, i)
                elif not (first and u == 0):
                    pe.wait_ge(attn_ready, n)
                for e in range(NE):
                    last = te.transpose(FF[:, P * e:P * (e + 1)], hr[:, D * e:D * (e + 1)], ident[:, :])
                last.then_inc(hT_done, 1)

            def mm2(done):
                pe.wait_ge(hT_ready, done)
                for e in range(NE):
                    last = te.matmul(FF[:, D * e:D * (e + 1)], hT[:, P * e:P * (e + 1)], w2_sb[:, D * e:D * (e + 1)],
                                     start=True, stop=True)
                last.then_inc(mm2_done, 1)

            def project(blocks):
                pe.wait_ge(attnT_ready, blocks)
                for q in range(GT):
                    last = te.matmul(FF[:, D * q:D * (q + 1)], attnT[:, P * q:P * (q + 1)], wproj_sb[:, :],
                                     start=True, stop=True)
                last.then_inc(proj_done, 1)

            def one_block(i, first):
                for u in range(NU):
                    n = i * NU + u
                    pe.wait_ge(operands_in[u % 2], i * (96 * NU // 2) + 96 * (u // 2 + 1))
                    for t in range(KT):
                        scores(i, u, t, 0, first)
                        scores(i, u, t, 1, first)
                        if t >= 2:
                            values(i, u, t - 2, first)
                        elif u:
                            values(i, u - 1, KT - 2 + t, first)
                        elif not first:
                            values(i - 1, NU - 1, KT - 2 + t, False)
                        if t == 1 and not (first and u == 0):
                            mm2(n)
                        if t == 2:
                            mm1(i, u, first)
                        if t == 3 and not (first and u == 0):
                            pe.wait_ge(h1_taken, n + 1)
                            pv_transpose(n)
                        if t == 5 and u == 0 and not first:
                            attn_transpose(n)
                        if t == 5 and u == 1 and not first:
                            pe.wait_ge(attn_ready, n)
                            project(i)
                        if t == 7:
                            h_transpose(i, u, first)

            one_block(0, True)
            with pe.Fori(1, NG) as i:
                one_block(i, False)
            for t in (KT - 2, KT - 1):
                values(NG - 1, NU - 1, t, False)
            mm2(NT)
            pe.wait_ge(y_taken, NT)
            pv_transpose(NT)
            attn_transpose(NT)
            project(NG)


_OUTS = [((B, S, D), "float32")]


def kernel(L0_attn_x, L0_attn_Wqkv, L0_attn_bqkv, L0_attn_Wproj, L0_attn_bproj, L0_attn_qn_w, L0_attn_kn_w,
           L0_ffn_gate_W, L0_ffn_gate_b, L0_ffn_W1, L0_ffn_b1, L0_ffn_g1, L0_ffn_be1, L0_ffn_W2, L0_ffn_b2,
           L0_ffn_g2, L0_ffn_be2):
    import concourse.bacc as bacc
    from concourse.bass_utils import run_bass_kernel_spmd

    def flat(*arrays):
        return np.concatenate([np.asarray(a).reshape(1, -1) for a in arrays], axis=1)

    wide = {
        "x": np.asarray(L0_attn_x),
        "wcat": np.concatenate([np.asarray(L0_attn_Wqkv).T, np.asarray(L0_ffn_gate_W)], axis=1),
        "w1": np.asarray(L0_ffn_W1).transpose(1, 0, 2).reshape(D, NE * D),
        "w2": np.asarray(L0_ffn_W2).transpose(1, 0, 2).reshape(D, NE * D),
        "wproj": np.asarray(L0_attn_Wproj).T,
        "row_a": flat(L0_attn_bqkv, L0_ffn_gate_b, L0_attn_qn_w, L0_attn_kn_w),
        "row_b": flat(L0_ffn_b1, L0_ffn_g1, L0_ffn_be1, L0_ffn_b2, L0_ffn_g2, L0_ffn_be2, L0_attn_bproj),
    }
    nc = bacc.Bacc("TRN2", target_bir_lowering=False, num_devices=1)
    arrays, args = {}, {}
    for name, a in wide.items():
        a = np.ascontiguousarray(a)
        arrays[f"in_{name}"] = a
        args[name] = nc.dram_tensor(f"in_{name}", a.shape, mybir.dt.from_np(a.dtype), kind="ExternalInput").ap()
    shape, dtype = _OUTS[0]
    out = nc.dram_tensor("out_0", shape, mybir.dt.from_np(np.dtype(dtype)), kind="ExternalOutput").ap()
    build(nc, out=out, **args)
    r = run_bass_kernel_spmd(nc, [arrays], core_ids=[0])
    return r.results[0]["out_0"]
```

```python
from contextlib import ExitStack

import numpy as np

import concourse.bass as bass
from concourse import mybir

F32 = mybir.dt.float32
BF16 = mybir.dt.bfloat16
I32 = mybir.dt.int32
ALU = mybir.AluOpType
ACT = mybir.ActivationFunctionType
AX_X = mybir.AxisListType.X

P = 128
B, S, D = 2, 1024, 128
H, HD = 16, 8
NE = 4
TOK = B * S
NT = TOK // P
GT = 4
GW = GT * P
NG = TOK // GW
GB = NG // B
UT = 2
UW = UT * P
NUNIT = TOK // UW
EARLY = NUNIT // B
LATE = NUNIT - EARLY
HP = 4
NU = H // HP
KT = S // P
STEPS = 2 * KT
PARTS = 3
QSLOT = 2 * PARTS - 1
QROWS = QSLOT * HD + PARTS
KROWS = PARTS * HD
PAIR = PARTS * KROWS
LN_LOTS = ((0, 2), (2, 8), (8, 12), (12, 16))
RING = 8
SBUFS = 3
BLOCK_STEPS = NU * STEPS
SBUF_OF = [k % SBUFS for k in range(BLOCK_STEPS - 1)] + [1]
assert BLOCK_STEPS % SBUFS == 1
QKV = 3 * D
WCAT = QKV + NE
VW = 32
LN_EPS = 1e-5
RMS_EPS = 1e-6
SCALE = HD ** -0.5
EXP_SAFE = 64.0
TWO_ONES = float(np.array([0x3F803F80], np.uint32).view(np.float32)[0])
STORES = 3 * 16
LOADS = 4 * 16
DVE_BEFORE = 105
DVE_BLOCK = 45
POOL_PREP = 5
POOL_BLOCK = 28


class Chain:

    def __init__(self, engine, sem, base):
        self.engine, self.sem, self.base, self.n = engine, sem, base, 0

    def link(self, instruction):
        self.n += 1
        instruction.then_inc(self.sem, 1)
        self.engine.wait_ge(self.sem, self.base + self.n)




def build(nc, x, wcat, w1, w2, wproj, row_a, row_b, out):
    with ExitStack() as ctx:
        def sb(name, shape, dt=F32):
            return ctx.enter_context(nc.sbuf_tensor(name, shape, dt))

        def sem(name):
            return ctx.enter_context(nc.semaphore(name))

        q_parts = nc.dram_tensor("q_parts", (NG, QROWS, H, GW), BF16).ap()
        k_parts = nc.dram_tensor("k_parts", (B, KROWS, H, S), BF16).ap()

        wcat_sb = sb("wcat_sb", [P, WCAT])
        w1_sb = sb("w1_sb", [P, NE * D])
        w2_sb = sb("w2_sb", [P, NE * D])
        wproj_sb = sb("wproj_sb", [P, D])
        rowa = sb("rowa", [P, WCAT + 2 * HD])
        rowb = sb("rowb", [P, 6 * NE * D + D])
        E = NE * D
        b1, g1, be1, b2, g2, be2 = (rowb[:, j * E:(j + 1) * E] for j in range(6))
        bproj = rowb[:, 6 * E:6 * E + D]
        ident = sb("ident", [P, P])
        ident16 = sb("ident16", [P, P], BF16)
        qkw = sb("qkw", [P, 2 * D])

        x_sb = sb("x_sb", [P, NT * D])
        xn = sb("xn", [P, NT * D])
        xnT = sb("xnT", [P, TOK])
        v_sb = sb("v_sb", [P, NT, D + NE])
        gate = sb("gate", [P, NT * D])
        gsc = sb("gsc", [P, NT, NE])
        wgt = sb("wgt", [P, NT * NE])

        stats = sb("stats", [P, NT, 6])
        mv = sb("mv", [P, NT, 2])
        rstd = sb("rstd", [P, NT])
        qk_b = sb("qk_b", [P, 2 + LATE, UT, 2 * D])
        qk_w = sb("qk_w", [P, 2, UT, 2 * D])
        qk_sq = sb("qk_sq", [P, 2, UT, 2 * D])
        qk_n = sb("qk_n", [P, 2, UT, 2 * D])
        qk_r = sb("qk_r", [P, 2, UT, 2 * D])
        ssum = sb("ssum", [P, NUNIT, UT * 2 * H])
        split = sb("split", [P, 2, PARTS, UT, 2 * D], BF16)
        splitT = sb("splitT", [P, 2, 2 * PARTS, UW], BF16)
        zero_rows = sb("zero_rows", [PARTS * H, TOK], BF16)
        tri = sb("tri", [P, NE, NE])
        cmp_gt = sb("cmp_gt", [P, NT, NE, NE])
        cmp_eq = sb("cmp_eq", [P, NT, NE, NE])
        rank = sb("rank", [P, NT, NE])
        gmax = sb("gmax", [P, NT])
        gexp = sb("gexp", [P, NT, NE])
        gsum = sb("gsum", [P, NT])

        k_op = sb("k_op", [P, 2, HP, S], BF16)
        q_op = sb("q_op", [P, 2, HP, GW], BF16)
        v_op = sb("v_op", [P, 2, KT, HP, VW])
        probs = sb("probs", [P, RING, 2 * GW])
        pv_sb = sb("pv_sb", [P, GW])
        rden = sb("rden", [P, GT, HP])
        attn = sb("attn", [P, GT, D])
        attnT = sb("attnT", [P, GW])

        xT_op = sb("xT_op", [P, 2, P])
        h1 = sb("h1", [P, E])
        st1 = sb("st1", [P, NE, 6])
        mv1 = sb("mv1", [P, NE, 2])
        ve1 = sb("ve1", [P, NE])
        rs1 = sb("rs1", [P, NE])
        hn = sb("hn", [P, E])
        hT = sb("hT", [P, E])
        y = sb("y", [P, E])
        st2 = sb("st2", [P, NE, 6])
        mv2 = sb("mv2", [P, NE, 2])
        ve2 = sb("ve2", [P, NE])
        rs2 = sb("rs2", [P, NE])
        rw2 = sb("rw2", [P, NE])
        z = sb("z", [P, E])
        wb = sb("wb", [P, E])
        wb2 = sb("wb2", [P, 2 * D])
        base = sb("base", [P, D])
        moe = sb("moe", [P, D])
        moe_t = sb("moe_t", [P, NE - 1, D])
        neg = sb("neg", [P, D])
        eneg = sb("eneg", [P, D])
        den = sb("den", [P, D])
        sig = sb("sig", [P, D])
        s_t = sb("s_t", [P, GW])
        o_sb = sb("o_sb", [P, GW])
        wprod = sb("wprod", [1, HD])
        wmax = sb("wmax", [1, 1])
        large = sb("large", [1, 1], I32)
        smax = sb("smax", [P, NT, H])
        shift = sb("shift", [P, NT, PARTS, H], BF16)

        eps = sb("eps", [P, 2])
        warm = sb("warm", [P, 2])
        half = sb("half", [P, NE])

        psum = ctx.enter_context(nc.psum_tensor("psum", [P, 8 * 512], F32))

        def bank(n, w=512):
            return psum[:, 512 * n:512 * n + w]

        in_x = [sem(f"in_x{j}") for j in range(len(LN_LOTS))]
        in_w = sem("in_w")
        in_wb = sem("in_wb")
        ident_ready = sem("ident_ready")
        cleared = sem("cleared")
        eps_ready = sem("eps_ready")
        dve_links = sem("dve_links")
        pool_links = sem("pool_links")
        dve_waits = sem("dve_waits")
        pool_waits = sem("pool_waits")
        lnvar_ready = sem("lnvar_ready")
        lnstd_ready = sem("lnstd_ready")
        xn_ready = sem("xn_ready")
        xT_done = sem("xT_done")
        xnT_ready = sem("xnT_ready")
        qkv_done = sem("qkv_done")
        v_taken = sem("v_taken")
        qk_ready = sem("qk_ready")
        sq_ready = sem("sq_ready")
        ss_ready = sem("ss_ready")
        rms_ready = sem("rms_ready")
        qkw_ready = sem("qkw_ready")
        qkn_ready = sem("qkn_ready")
        hi_ready = sem("hi_ready")
        res_ready = sem("res_ready")
        mid_ready = sem("mid_ready")
        lo_ready = sem("lo_ready")
        partsT_done = sem("partsT_done")
        partsT_dve = sem("partsT_dve")
        partsT_act = sem("partsT_act")
        lateT_done = sem("lateT_done")
        lateT_taken = sem("lateT_taken")
        stored = [sem(f"stored{g}") for g in range(2)]
        shift_zeroed = sem("shift_zeroed")
        gdiff_ready = sem("gdiff_ready")
        gexp_ready = sem("gexp_ready")
        wgt_ready = sem("wgt_ready")

        large_ready = sem("large_ready")
        max_operands_in = sem("max_operands_in")
        max_scores_done = sem("max_scores_done")
        max_taken = sem("max_taken")
        max_links = sem("max_links")
        shift_ready = sem("shift_ready")
        shiftT_done = sem("shiftT_done")
        shift_rows_ready = sem("shift_rows_ready")
        shift_stored = sem("shift_stored")

        first_k_in = [sem(f"first_k_in{j}") for j in range(2)]
        first_q_in = sem("first_q_in")
        first_again_in = sem("first_again_in")
        operands_in = [sem(f"operands_in{j}") for j in range(2)]
        scores_done = sem("scores_done")
        probs_ready = sem("probs_ready")
        pv_done = sem("pv_done")
        staged = sem("staged")
        pv_taken = sem("pv_taken")
        pvT_done = sem("pvT_done")
        attn_ready = sem("attn_ready")
        attnT_done = sem("attnT_done")
        attnT_ready = sem("attnT_ready")
        mm1_done = sem("mm1_done")
        h1_taken = sem("h1_taken")
        mv1_ready = sem("mv1_ready")
        rs1_ready = sem("rs1_ready")
        hn_ready = sem("hn_ready")
        hg_ready = sem("hg_ready")
        hr_ready = sem("hr_ready")
        hT_done = sem("hT_done")
        hT_ready = sem("hT_ready")
        mm2_done = sem("mm2_done")
        y_taken = sem("y_taken")
        mv2_ready = sem("mv2_ready")
        rs2_ready = sem("rs2_ready")
        base_ready = sem("base_ready")
        neg_ready = sem("neg_ready")
        eneg_ready = sem("eneg_ready")
        proj_done = sem("proj_done")
        proj_taken = sem("proj_taken")
        out_ready = sem("out_ready")
        out_stored = sem("out_stored")

        x_v = x.rearrange("b (t p) d -> p (b t) d", p=P)
        out_v = out.rearrange("b (t p) d -> p (b t) d", p=P)
        x_3 = x_sb[:, :].rearrange("p (t d) -> p t d", d=D)

        def xT_ps(g):
            return bank(g % 2, UW)

        def qkv_ps(g):
            return psum[:, 512 * (2 + 2 * (g % 2)):512 * (4 + 2 * (g % 2))].rearrange("p (t c) -> p t c", t=UT)

        parts_ps = psum[:, 512 * 6:512 * 8].bitcast(BF16)[:, 0:2 * PARTS * UW].rearrange(
            "p (s t c) -> p s t c", s=2 * PARTS, t=UT)

        def qkb(g):
            return qk_b[:, g % 2 if g < EARLY else 2 + g - EARLY, :, :]

        def qkw_out(g):
            return qk_w[:, g % 2, :, :] if g < EARLY else qkb(g)

        late_ps = psum[:, 512 * 7:512 * 8].bitcast(BF16)[:, 0:2 * PARTS * P].rearrange("p (s c) -> p s c", s=2 * PARTS)
        PV, FF = bank(6), bank(7)

        MAXN = HP * GT
        CREDIT = 2

        def scores_may_be_large(engine):
            engine.wait_ge(large_ready, 1)
            return engine.value_load(large[0:1, 0:1], min_val=0, max_val=1) > 0

        block = ctx.enter_context(nc.Block())

        @block.sync
        def _(sp):
            def load_x(lot):
                lo, hi = LN_LOTS[lot]
                sp.dma_start(x_3[:, lo:hi, :], x_v[:, lo:hi, :]).then_inc(in_x[lot], 16)

            load_x(0)
            sp.dma_start(wcat_sb[:, :], wcat).then_inc(in_w, 16)
            load_x(1)
            sp.dma_start(rowa[:, :], row_a.broadcast_to([P, WCAT + 2 * HD])).then_inc(in_w, 16)
            load_x(2)
            load_x(3)
            sp.dma_start(w1_sb[:, :], w1).then_inc(in_wb, 16)
            sp.dma_start(w2_sb[:, :], w2).then_inc(in_wb, 16)
            sp.dma_start(wproj_sb[:, :], wproj).then_inc(in_wb, 16)
            sp.dma_start(rowb[:, :], row_b.broadcast_to([P, 6 * E + D])).then_inc(in_wb, 16)

            def store_parts(g):
                q_cols = slice(UW * g % GW, UW * g % GW + UW)
                k_cols = slice(UW * g % S, UW * g % S + UW)
                for lo, n in ((0, PARTS), (PARTS, QSLOT - PARTS)):
                    sp.dma_start(q_parts[UW * g // GW, lo * HD:(lo + n) * HD, :, q_cols].rearrange(
                        "(s d) h t -> (d h) s t", d=HD), splitT[:, g % 2, 0:n, :]).then_inc(stored[g % 2], 16)
                sp.dma_start(k_parts[UW * g // S, :, :, k_cols].rearrange("(s d) h t -> (d h) s t", d=HD),
                             splitT[:, g % 2, PARTS:2 * PARTS, :]).then_inc(stored[g % 2], 16)

            def store_shifts(lo, hi):
                return sp.dma_start(q_parts[lo:hi, QSLOT * HD:, :, :].rearrange("g s h t -> (s h) g t"),
                                    zero_rows[:, GW * lo:GW * hi].rearrange("p (g t) -> p g t", t=GW))

            def store_late(g):
                sp.wait_ge(lateT_taken, UT * (g + 1 - EARLY))
                store_parts(g)

            def load_q(i, u, par, arrived):
                for a in range(PARTS):
                    rows = KROWS + (PARTS if a == PARTS - 1 else 0)
                    sp.dma_start(q_op[KROWS * a:KROWS * a + rows, par, :, :].rearrange("r h t -> r (h t)"),
                                 q_parts[bass.ds(i, 1), HD * a:HD * a + rows, HP * u:HP * (u + 1), :].rearrange(
                                     "g r h t -> r (g h t)")).then_inc(arrived, 16)

            def load_first_k(half):
                cols = slice(half * S // 2, (half + 1) * S // 2)
                for a in range(PARTS):
                    sp.dma_start(k_op[KROWS * a:KROWS * (a + 1), 0, :, cols],
                                 k_parts[0, :, 0:HP, cols]).then_inc(first_k_in[half], 16)

            for g in range(EARLY):
                sp.wait_ge(partsT_dve, g + 1)
                sp.wait_ge(partsT_act, g + 1)
                store_parts(g)
                if g == 0:
                    sp.wait_ge(cleared, 1)
                    store_shifts(0, NG).then_inc(shift_zeroed, 16)
                if g == EARLY // 2 - 1:
                    for par in range(2):
                        sp.wait_ge(stored[par], STORES * EARLY // 4)
                    sp.wait_ge(shift_zeroed, 16)
                    sp.wait_ge(cleared, 3)
                    load_first_k(0)
                    load_q(0, 0, 0, first_q_in)

            def operand_dmas(i, u, par, arrived):
                heads = slice(HP * u, HP * (u + 1))
                k_rows = k_parts[bass.ds(i // GB, 1), :, heads, :].rearrange("b r h t -> r (b h t)")
                sp.dma_start(k_op[0:PAIR, par, :, :].rearrange("r h t -> r (h t)"),
                             k_rows.unsqueeze(0).broadcast_to([PARTS, KROWS, HP * S])).then_inc(arrived, 16)
                load_q(i, u, par, arrived)

            def load_operands(i, u, first):
                par = u % 2
                if not (first and u < 2):
                    sp.wait_ge(scores_done, i * NU * STEPS + STEPS * (u - 1))
                operand_dmas(i, u, par, operands_in[par])

            def store_block(i, count):
                sp.wait_ge(out_ready, count)
                sp.dma_start(out_v[:, bass.ds(i * GT, GT), :], o_sb[:, :].rearrange("p (t d) -> p t d", d=D)).then_inc(
                    out_stored, 16)

            large_scores = scores_may_be_large(sp)

            def shifts(b):
                with sp.If(large_scores):
                    if b == 0:
                        for half in range(2):
                            sp.wait_ge(first_k_in[half], 16 * PARTS)
                        sp.wait_ge(first_q_in, 16 * PARTS)
                    with sp.Fori(GB * b, GB * (b + 1)) as i:
                        for u in range(NU):
                            sp.wait_ge(max_taken, (i * NU + u) * MAXN + CREDIT)
                            operand_dmas(i, u, 0, max_operands_in)
                    sp.wait_ge(shift_rows_ready, b + 1)
                    store_shifts(GB * b, GB * (b + 1)).then_inc(shift_stored, 16)
                    sp.wait_ge(shift_stored, 16 * (b + 1))
                    if b == 0:
                        operand_dmas(0, 0, 0, first_again_in)

            for par in range(2):
                sp.wait_ge(stored[par], STORES * EARLY // 2)
            load_first_k(1)
            shifts(0)
            load_operands(0, 1, True)
            store_late(EARLY)
            load_operands(0, 2, True)
            store_late(EARLY + 1)
            load_operands(0, 3, True)
            store_late(EARLY + 2)
            load_operands(1, 0, False)
            store_late(EARLY + 3)
            for u in range(1, NU):
                load_operands(1, u, False)
            for par in range(2):
                sp.wait_ge(stored[par], STORES * NUNIT // 2)
            sp.wait_ge(scores_done, (GB * NU - 1) * STEPS)
            shifts(1)
            with sp.Fori(2, NG) as i:
                for u in range(NU):
                    load_operands(i, u, False)
                    if u == 0:
                        store_block(i - 2, i - 1)
            store_block(NG - 2, NG - 1)
            store_block(NG - 1, NG)
            sp.wait_ge(out_stored, 16 * NG)

        @block.gpsimd
        def _(pool):
            gp = nc.gpsimd
            ch = Chain(pool, pool_links, 0)
            ch.link(gp.memset(ident[:], 0.0))
            ch.link(gp.affine_select(out=ident[:, :], in_=ident[:, :], compare_op=ALU.not_equal, fill=1.0,
                                     base=0, pattern=[[-1, P]], channel_multiplier=1))
            gp.tensor_copy(ident16[:, :], ident[:, :]).then_inc(ident_ready, 1)
            gp.memset(half[:], -0.5)
            gp.memset(zero_rows[:, :].bitcast(F32), 0.0).then_inc(cleared, 1)
            pool.wait_ge(cleared, 1)
            gp.memset(q_op[:, :, :, :].bitcast(F32), 0.0).then_inc(cleared, 1)
            pool.wait_ge(cleared, 2)
            gp.memset(k_op[:, :, :, :].bitcast(F32), TWO_ONES).then_inc(cleared, 1)
            ch.link(gp.memset(v_op[:], 0.0))
            ch.link(gp.memset(v_op[:, :, :, :, HD:HD + 1], 1.0))
            pool.wait_ge(in_w, 32)
            qn = rowa[:, WCAT:WCAT + HD]
            kn = rowa[:, WCAT + HD:WCAT + 2 * HD]
            gp.tensor_scalar(qkw[:, 0:D].rearrange("p (h d) -> p h d", d=HD),
                             qn.unsqueeze(1).broadcast_to([P, H, HD]), SCALE, 1.0, ALU.mult, ALU.mult)
            ch.link(gp.tensor_scalar(qkw[:, D:2 * D].rearrange("p (h d) -> p h d", d=HD),
                                     kn.unsqueeze(1).broadcast_to([P, H, HD]), 1.0, 1.0, ALU.mult, ALU.mult))

            def weigh(g):
                pool.wait_ge(qk_ready, g + 1)
                if g >= EARLY:
                    pool.wait_ge(sq_ready, g + 1)
                elif g >= 2:
                    pool.wait_ge(qkn_ready, g - 1)
                gp.tensor_tensor(qkw_out(g), qkb(g), qkw[:, :].unsqueeze(1).broadcast_to([P, UT, 2 * D]),
                                 ALU.mult).then_inc(qkw_ready, 1)

            for g in range(EARLY):
                weigh(g)
                if g:
                    pool.wait_ge(mid_ready, g)
                    if g >= 3:
                        pool.wait_ge(partsT_done, g - 2)
                    gp.tensor_tensor(split[:, (g - 1) % 2, 2, :, :], qk_r[:, (g - 1) % 2, :, :],
                                     split[:, (g - 1) % 2, 1, :, :], ALU.subtract).then_inc(lo_ready, 1)
            assert ch.n == POOL_PREP, ("POOL_PREP", ch.n)

            def hi_late(g):
                if g - 2 < EARLY:
                    pool.wait_ge(partsT_done, g - 1)
                else:
                    pool.wait_ge(lateT_done, UT * (g - 1 - EARLY))
                pool.wait_ge(qkn_ready, g + 1)
                gp.tensor_copy(split[:, g % 2, 0, :, :], qk_n[:, g % 2, :, :]).then_inc(hi_ready, 1)

            def mid_late(g):
                pool.wait_ge(res_ready, g + 1)
                gp.tensor_copy(split[:, g % 2, 1, :, :], qk_r[:, g % 2, :, :]).then_inc(mid_ready, 1)

            def stage(i, u):
                pool.sem_inc(pool_waits, 1)
                v_b = v_sb[:, bass.ds((i // 2) * KT, KT), :]
                heads = slice(HP * HD * u, HP * HD * (u + 1))
                v_bias = rowa[:, 2 * D:QKV][:, heads].rearrange("p (h d) -> p h d", d=HD)
                gp.tensor_tensor(v_op[:, u % 2, :, :, 0:HD],
                                 v_b[:, :, heads].rearrange("p t (h d) -> p t h d", d=HD),
                                 v_bias.unsqueeze(1).broadcast_to([P, KT, HP, HD]), ALU.add).then_inc(staged, 1)
                gp.tensor_copy(xT_op[:, u % 2, :], xnT[:, bass.ds(i * GW + u * P, P)]).then_inc(staged, 1)

            def inverse_std(ch, dst, tmp, mv_):
                pool.sem_inc(pool_waits, 1)
                ch.link(gp.tensor_scalar(tmp[:, :], mv_[:, :, 1], LN_EPS, 1.0, ALU.add, ALU.mult))
                return gp.tensor_tensor(dst[:, :], tmp[:, :], half[:, :], ALU.pow)

            def second_factor(i, u, ch, prev):
                pool.wait_ge(mv2_ready, prev)
                ch.link(inverse_std(ch, rs2, ve2, mv2))
                pool.sem_inc(pool_waits, 1)
                gp.tensor_tensor(rw2[:, :], rs2[:, :], wgt[:, bass.ds((i * NU + u) * NE, NE)],
                                 ALU.mult).then_inc(rs2_ready, 1)

            def base_sum(i, u, ch):
                pool.sem_inc(pool_waits, 1)
                w = wgt[:, bass.ds((i * NU + u) * NE, NE)].unsqueeze(2).broadcast_to([P, NE, D])
                ch.link(gp.tensor_tensor(wb[:, :].rearrange("p (e d) -> p e d", e=NE),
                                         be2.rearrange("p (e d) -> p e d", e=NE), w, ALU.mult))
                ch.link(gp.tensor_tensor(wb2[:, :], wb[:, 0:2 * D], wb[:, 2 * D:4 * D], ALU.add))
                ch.link(gp.tensor_tensor(wb[:, 0:D], wb2[:, 0:D], wb2[:, D:2 * D], ALU.add))
                pool.sem_inc(pool_waits, 1)
                gp.tensor_tensor(base[:, :], wb[:, 0:D], xn[:, bass.ds((i * NU + u) * D, D)],
                                 ALU.add).then_inc(base_ready, 1)

            def one_block(i, ch, first, last):
                for u in range(NU):
                    n = i * NU + u
                    if not (first and u == 0):
                        second_factor(i if u else i - 1, (u - 1) % NU, ch, n)
                    if not (first and u == 0) and not (last and u == NU - 1):
                        pool.wait_ge(pv_done, i * NU * KT + KT * u)
                        stage(i if u < NU - 1 else i + 1, (u + 1) % NU)
                    pool.wait_ge(mv1_ready, n + 1)
                    inverse_std(ch, rs1, ve1, mv1).then_inc(rs1_ready, 1)
                    if first and u == 0:
                        mid_late(EARLY)
                    pool.wait_ge(hn_ready, n + 1)
                    ch.link(gp.tensor_tensor(hn[:, :], hn[:, :], g1, ALU.mult))
                    gp.tensor_tensor(hn[:, :], hn[:, :], be1, ALU.add).then_inc(hg_ready, 1)
                    if first and u == 0:
                        stage(0, 1)
                    if first and u + 1 < LATE:
                        hi_late(EARLY + 1 + u)
                        mid_late(EARLY + 1 + u)
                    if first and u == 0:
                        pool.wait_ge(wgt_ready, 1)
                    else:
                        pool.wait_ge(neg_ready, n)
                    base_sum(i, u, ch)

            pool.wait_ge(v_taken, EARLY)
            pool.wait_ge(xnT_ready, 1)
            stage(0, 0)
            for g in range(EARLY, NUNIT):
                weigh(g)
            hi_late(EARLY)
            pool.wait_ge(in_wb, 64)
            c0 = Chain(pool, pool_links, POOL_PREP)
            one_block(0, c0, True, False)
            assert c0.n == POOL_BLOCK - 2, ("POOL_BLOCK", c0.n + 2)
            with pool.Fori(1, NG - 1) as i:
                ci = Chain(pool, pool_links, (i - 1) * POOL_BLOCK + (POOL_PREP + POOL_BLOCK - 2))
                one_block(i, ci, False, False)
                assert ci.n == POOL_BLOCK, ("POOL_BLOCK", ci.n)
            cl = Chain(pool, pool_links, POOL_PREP + (NG - 1) * POOL_BLOCK - 2)
            one_block(NG - 1, cl, False, True)
            second_factor(NG - 1, NU - 1, cl, NT)

        @block.scalar
        def _(act):
            sc = nc.scalar

            act.wait_ge(eps_ready, 1)
            sc.activation(warm[:, :], eps[:, :], ACT.Sqrt)

            def ln_std(lot):
                lo, hi = LN_LOTS[lot]
                act.wait_ge(lnvar_ready, lot + 1)
                sc.activation(rstd[:, lo:hi], mv[:, lo:hi, 1], ACT.Sqrt, bias=eps[:, 0:1]).then_inc(lnstd_ready, 1)

            def copy_xT(g):
                act.wait_ge(xT_done, g + 1)
                sc.activation(xnT[:, UW * g:UW * (g + 1)], xT_ps(g), ACT.Copy).then_inc(xnT_ready, 1)

            def mid_part(g):
                act.wait_ge(res_ready, g + 1)
                sc.activation(split[:, g % 2, 1, :, :], qk_r[:, g % 2, :, :], ACT.Copy).then_inc(mid_ready, 1)

            def copy_parts(g):
                act.wait_ge(partsT_done, g + 1)
                if g >= 2:
                    act.wait_ge(stored[g % 2], STORES * (g // 2))
                sc.activation(splitT[:, g % 2, 4:6, :], parts_ps[:, 4:6, :, :], ACT.Copy).then_inc(partsT_act, 1)

            def take_v(g):
                act.wait_ge(qkv_done, g + 1)
                sc.activation(v_sb[:, UT * g:UT * (g + 1), :], qkv_ps(g)[:, :, 2 * D:WCAT],
                              ACT.Copy).then_inc(v_taken, 1)

            def square(g):
                act.wait_ge(qk_ready, g + 1)
                if g >= 2:
                    act.wait_ge(ss_ready, g - 1)
                sc.activation(qk_sq[:, g % 2, :, :], qkb(g), ACT.Square).then_inc(sq_ready, 1)

            ln_std(0)
            copy_xT(0)
            ln_std(1)
            copy_xT(1)
            for g in range(EARLY):
                square(g)
                take_v(g)
                if g:
                    mid_part(g - 1)
                if g >= 2:
                    copy_parts(g - 2)
                act.wait_ge(ss_ready, g + 1)
                sc.activation(ssum[:, g, :], ssum[:, g, :], ACT.Sqrt, bias=eps[:, 1:2],
                              scale=1.0 / HD).then_inc(rms_ready, 1)
                if g + 2 < EARLY:
                    copy_xT(g + 2)
                if g == EARLY - 1:
                    ln_std(2)
                    copy_xT(EARLY)
                act.wait_ge(qkn_ready, g + 1)
                if g >= 2:
                    act.wait_ge(partsT_done, g - 1)
                sc.activation(split[:, g % 2, 0, :, :], qk_n[:, g % 2, :, :], ACT.Copy).then_inc(hi_ready, 1)
            mid_part(EARLY - 1)
            copy_parts(EARLY - 2)
            copy_xT(EARLY + 1)
            ln_std(3)
            square(EARLY)
            take_v(EARLY)
            copy_parts(EARLY - 1)
            copy_xT(EARLY + 2)
            copy_xT(EARLY + 3)
            for g in range(EARLY + 1, NUNIT):
                square(g)
                take_v(g)
            act.wait_ge(ss_ready, NUNIT)
            sc.activation(ssum[:, EARLY:, :], ssum[:, EARLY:, :], ACT.Sqrt, bias=eps[:, 1:2],
                          scale=1.0 / HD).then_inc(rms_ready, 1)

            def exp_step(i, k, first):
                n = i * NU * STEPS + k
                act.wait_ge(scores_done, n + 1)
                if not (first and k < RING):
                    act.wait_ge(pv_done, i * NU * KT + (k - RING) // 2 + 1)
                sc.activation(probs[:, k % RING, :], bank(2 * SBUF_OF[k], 2 * GW),
                              ACT.Exp).then_inc(probs_ready, 1)

            def exp_neg(count):
                act.wait_ge(neg_ready, count)
                sc.activation(eneg[:, :], neg[:, :], ACT.Exp).then_inc(eneg_ready, 1)

            def one_block(i, first):
                for u in range(NU):
                    for k in range(STEPS):
                        exp_step(i, u * STEPS + k, first)
                        if k == STEPS - 2 and not (first and u == 0):
                            exp_neg(i * NU + u)
                        elif k == STEPS - 2:
                            act.wait_ge(gdiff_ready, 1)
                            sc.activation(gexp[:, :, :], gexp[:, :, :], ACT.Exp).then_inc(gexp_ready, 1)

            one_block(0, True)
            with act.Fori(1, NG) as i:
                one_block(i, False)
            exp_neg(NT)

        @block.vector
        def _(dve):
            ve = nc.vector
            ch = Chain(dve, dve_links, 0)

            def ln_stats(lot):
                lo, hi = LN_LOTS[lot]
                dve.wait_ge(in_x[lot], 16)
                for t in range(lo, hi):
                    st = ve.bn_stats(stats[:, t, :], x_3[:, t, :])
                ch.link(st)
                for t in range(lo, hi):
                    st = ve.bn_aggr(mv[:, t, :], stats[:, t, :])
                st.then_inc(lnvar_ready, 1)

            def ln_recip(lot):
                lo, hi = LN_LOTS[lot]
                dve.wait_ge(lnstd_ready, lot + 1)
                ch.link(ve.reciprocal(rstd[:, lo:hi], rstd[:, lo:hi]))

            def ln_apply(g):
                for t in range(UT * g, UT * (g + 1)):
                    last = ve.tensor_scalar(xn[:, D * t:D * (t + 1)], x_sb[:, D * t:D * (t + 1)], mv[:, t, 0:1],
                                            rstd[:, t:t + 1], ALU.subtract, ALU.mult)
                last.then_inc(xn_ready, 1)

            bias = rowa[:, 0:WCAT]
            ve.memset(eps[:, 0:1], LN_EPS)
            ve.memset(eps[:, 1:2], RMS_EPS).then_inc(eps_ready, 1)
            for e in range(1, NE):
                ve.memset(tri[:, e, 0:e], 1.0)
            for e in range(NE):
                st = ve.memset(tri[:, e, e:NE], 0.0)
            ch.link(st)
            ln_stats(0)
            ln_recip(0)
            ln_apply(0)
            ln_stats(1)
            ln_recip(1)
            ln_apply(1)
            dve.wait_ge(in_w, 32)
            ch.link(ve.tensor_tensor(wprod[:, :], rowa[0:1, WCAT:WCAT + HD], rowa[0:1, WCAT + HD:WCAT + 2 * HD],
                                     ALU.mult))
            ch.link(ve.tensor_tensor(wprod[:, :], wprod[:, :], wprod[:, :], ALU.mult))
            ch.link(ve.tensor_reduce(wmax[:, :], wprod[:, :], AX_X, ALU.max))
            ve.tensor_scalar(large[:, :], wmax[:, :], (EXP_SAFE / (SCALE * HD)) ** 2, None,
                             ALU.is_gt).then_inc(large_ready, 1)

            def take_qkv(g):
                dve.wait_ge(qkv_done, g + 1)
                if 2 <= g < EARLY:
                    dve.wait_ge(qkw_ready, g - 1)
                    dve.wait_ge(sq_ready, g - 1)
                ve.tensor_tensor(qkb(g), qkv_ps(g)[:, :, 0:2 * D],
                                 bias[:, 0:2 * D].unsqueeze(1).broadcast_to([P, UT, 2 * D]),
                                 ALU.add).then_inc(qk_ready, 1)

            def square_sum(g):
                dve.wait_ge(sq_ready, g + 1)
                ve.tensor_reduce(ssum[:, g, :], qk_sq[:, g % 2, :, :].rearrange("p t (h d) -> p (t h) d", d=HD),
                                 AX_X, ALU.add).then_inc(ss_ready, 1)

            def rms_apply(g):
                if g < EARLY:
                    dve.wait_ge(rms_ready, g + 1)
                    ch.link(ve.reciprocal(ssum[:, g, :], ssum[:, g, :]))
                dve.wait_ge(qkw_ready, g + 1)
                ve.tensor_tensor(
                    qk_n[:, g % 2, :, :].rearrange("p t (x d h) -> p (t x) h d", x=2, d=HD),
                    qkw_out(g).rearrange("p t (x h d) -> p (t x) h d", x=2, d=HD),
                    ssum[:, g, :].rearrange("p (y h) -> p y h", h=H).unsqueeze(3)
                    .broadcast_to([P, UT * 2, H, HD]), ALU.mult).then_inc(qkn_ready, 1)

            def residue(g):
                dve.wait_ge(hi_ready, g + 1)
                ve.tensor_tensor(qk_r[:, g % 2, :, :], qk_n[:, g % 2, :, :], split[:, g % 2, 0, :, :],
                                 ALU.subtract).then_inc(res_ready, 1)

            def lo_part(g):
                dve.wait_ge(mid_ready, g + 1)
                ve.tensor_tensor(split[:, g % 2, 2, :, :], qk_r[:, g % 2, :, :], split[:, g % 2, 1, :, :],
                                 ALU.subtract).then_inc(lo_ready, 1)

            def copy_parts(g):
                dve.wait_ge(partsT_done, g + 1)
                if g >= 2:
                    dve.wait_ge(stored[g % 2], STORES * (g // 2))
                ve.tensor_copy(splitT[:, g % 2, 0:4, :], parts_ps[:, 0:4, :, :]).then_inc(partsT_dve, 1)

            for g in range(EARLY):
                take_qkv(g)
                if g >= 2:
                    copy_parts(g - 2)
                if g:
                    residue(g - 1)
                square_sum(g)
                if g + 2 < EARLY:
                    ln_apply(g + 2)
                if g == EARLY - 1:
                    ln_stats(2)
                    ln_recip(2)
                    ln_apply(EARLY)
                rms_apply(g)
            residue(EARLY - 1)
            copy_parts(EARLY - 2)
            ln_apply(EARLY + 1)
            lo_part(EARLY - 1)
            ln_stats(3)
            take_qkv(EARLY)
            copy_parts(EARLY - 1)
            ln_recip(3)
            ln_apply(EARLY + 2)
            ln_apply(EARLY + 3)
            take_qkv(EARLY + 1)
            square_sum(EARLY)
            square_sum(EARLY + 1)
            take_qkv(EARLY + 2)
            take_qkv(EARLY + 3)
            square_sum(EARLY + 2)
            square_sum(EARLY + 3)

            def gate_ranks():
                of_f = gsc[:, :, :].unsqueeze(2).broadcast_to([P, NT, NE, NE])
                of_e = gsc[:, :, :].unsqueeze(3).broadcast_to([P, NT, NE, NE])
                flat = "p t e f -> p t (e f)"
                dve.wait_ge(v_taken, NUNIT)
                ch.link(ve.tensor_tensor(gsc[:, :, :], v_sb[:, :, D:D + NE],
                                         bias[:, QKV:WCAT].unsqueeze(1).broadcast_to([P, NT, NE]), ALU.add))
                ve.tensor_reduce(gmax[:, :], gsc[:, :, :], AX_X, ALU.max)
                ve.tensor_tensor(cmp_gt[:, :, :, :], of_f, of_e, ALU.is_gt)
                ch.link(ve.tensor_tensor(cmp_eq[:, :, :, :], of_f, of_e, ALU.is_equal))
                ve.tensor_tensor(gexp[:, :, :], gsc[:, :, :], gmax[:, :].unsqueeze(2).broadcast_to([P, NT, NE]),
                                 ALU.subtract).then_inc(gdiff_ready, 1)
                ch.link(ve.tensor_tensor(cmp_eq[:, :, :, :].rearrange(flat), cmp_eq[:, :, :, :].rearrange(flat),
                                         tri[:, :, :].rearrange("p e f -> p (e f)").unsqueeze(1)
                                         .broadcast_to([P, NT, NE * NE]), ALU.mult))
                ch.link(ve.tensor_tensor(cmp_gt[:, :, :, :], cmp_gt[:, :, :, :], cmp_eq[:, :, :, :], ALU.add))
                ch.link(ve.tensor_reduce(rank[:, :, :], cmp_gt[:, :, :, :], AX_X, ALU.add))
                ch.link(ve.tensor_scalar(rank[:, :, :], rank[:, :, :], 1.5, None, ALU.is_lt))

            def gate_weights():
                dve.wait_ge(gexp_ready, 1)
                ch.link(ve.tensor_tensor(gexp[:, :, :], gexp[:, :, :], rank[:, :, :], ALU.mult))
                ch.link(ve.tensor_reduce(gsum[:, :], gexp[:, :, :], AX_X, ALU.add))
                ch.link(ve.reciprocal(gsum[:, :], gsum[:, :]))
                ve.tensor_tensor(wgt[:, :].rearrange("p (t e) -> p t e", e=NE), gexp[:, :, :],
                                 gsum[:, :].unsqueeze(2).broadcast_to([P, NT, NE]), ALU.mult).then_inc(wgt_ready, 1)
                dve.wait_ge(wgt_ready, 1)

            large_scores = scores_may_be_large(dve)

            def maxima(b):
                tiles = slice(KT * b, KT * (b + 1))
                with dve.If(large_scores):
                    if b == 0:
                        dve.sem_inc(max_taken, CREDIT)
                    with dve.Fori(GB * b, GB * (b + 1)) as i:
                        for u in range(NU):
                            for m in range(MAXN):
                                head, q = HP * u + m // GT, m % GT
                                dve.wait_ge(max_scores_done, (i * NU + u) * MAXN + m + 1)
                                dve.sem_inc(dve_waits, 1)
                                ve.tensor_reduce(smax[:, bass.ds(i * GT + q, 1), head], bank(2 * (m % 2), 2 * GW),
                                                 AX_X, ALU.max).then_inc(max_taken, 1)
                    dve.wait_ge(max_taken, GB * (b + 1) * NU * MAXN + CREDIT)
                    cm = Chain(dve, max_links, 4 * b)
                    cm.link(ve.tensor_scalar(smax[:, tiles, :], smax[:, tiles, :], -1.0, None, ALU.mult))
                    cm.link(ve.tensor_copy(shift[:, tiles, 0, :], smax[:, tiles, :]))
                    cm.link(ve.tensor_tensor(smax[:, tiles, :], smax[:, tiles, :], shift[:, tiles, 0, :],
                                             ALU.subtract))
                    cm.link(ve.tensor_copy(shift[:, tiles, 1, :], smax[:, tiles, :]))
                    assert cm.n == 4
                    ve.tensor_tensor(shift[:, tiles, 2, :], smax[:, tiles, :], shift[:, tiles, 1, :],
                                     ALU.subtract).then_inc(shift_ready, 1)
                    dve.wait_ge(shiftT_done, b + 1)
                    dve.wait_ge(shift_zeroed, 16)
                    ve.tensor_copy(zero_rows[:, S * b:S * (b + 1)],
                                   psum[0:H * PARTS, 0:GW].bitcast(BF16)).then_inc(shift_rows_ready, 1)

            maxima(0)
            dve.wait_ge(rms_ready, EARLY + 1)
            ch.link(ve.reciprocal(ssum[:, EARLY:, :], ssum[:, EARLY:, :]))
            rms_apply(EARLY)
            dve.wait_ge(in_wb, 64)

            def col(e):
                return slice(D * e, D * (e + 1))

            def take_y(n_done, ch, between=None):
                dve.wait_ge(mm2_done, n_done)
                ve.tensor_tensor(y[:, :], FF, b2, ALU.add).then_inc(y_taken, 1)
                if between:
                    between(n_done)
                dve.wait_ge(y_taken, n_done)
                for e in range(NE):
                    st = ve.bn_stats(st2[:, e, :], y[:, col(e)])
                ch.link(st)
                dve.sem_inc(dve_waits, 1)
                for e in range(NE):
                    st = ve.bn_aggr(mv2[:, e, :], st2[:, e, :])
                st.then_inc(mv2_ready, 1)
                dve.wait_ge(mv2_ready, n_done)

            def take_h(n_done, ch):
                dve.wait_ge(mm1_done, n_done)
                ve.tensor_tensor(h1[:, :], FF, b1, ALU.add).then_inc(h1_taken, 1)
                dve.wait_ge(h1_taken, n_done)
                for e in range(NE):
                    st = ve.bn_stats(st1[:, e, :], h1[:, col(e)])
                ch.link(st)
                dve.sem_inc(dve_waits, 1)
                for e in range(NE):
                    st = ve.bn_aggr(mv1[:, e, :], st1[:, e, :])
                st.then_inc(mv1_ready, 1)

            def normalize(dst, src, mv_, rs, done):
                for e in range(NE):
                    st = ve.tensor_scalar(dst[:, col(e)], src[:, col(e)], mv_[:, e, 0:1], rs[:, e:e + 1],
                                          ALU.subtract, ALU.mult)
                st.then_inc(done, 1)

            def centre_y(ch):
                for e in range(NE):
                    st = ve.scalar_tensor_tensor(z[:, col(e)], y[:, col(e)], mv2[:, e, 0:1], g2[:, col(e)],
                                                 ALU.subtract, ALU.mult)
                ch.link(st)

            def mix(n_done, ch):
                dve.wait_ge(rs2_ready, n_done)
                dve.wait_ge(base_ready, n_done)
                dve.sem_inc(dve_waits, 1)
                total = base[:, :]
                for e in range(NE):
                    dst = moe_t[:, e, :] if e < NE - 1 else moe[:, :]
                    ch.link(ve.scalar_tensor_tensor(dst, z[:, col(e)], rw2[:, e:e + 1], total, ALU.mult, ALU.add))
                    total = dst
                ve.tensor_scalar(neg[:, :], moe[:, :], -1.0, 87.0, ALU.mult, ALU.min).then_inc(neg_ready, 1)

            def silu(i, u, n_done, ch):
                dve.wait_ge(eneg_ready, n_done)
                ch.link(ve.tensor_scalar(den[:, :], eneg[:, :], 1.0, None, ALU.add))
                ch.link(ve.reciprocal(sig[:, :], den[:, :]))
                ch.link(ve.tensor_tensor(gate[:, bass.ds((i * NU + u) * D, D)], moe[:, :], sig[:, :], ALU.mult))

            def take_pv(passes):
                dve.wait_ge(pv_done, KT * passes)
                ve.tensor_copy(pv_sb[:, :], PV).then_inc(pv_taken, 1)

            def divide(passes, u, ch):
                dve.wait_ge(pvT_done, passes)
                pvT = FF.rearrange("p (q h c) -> p q h c", q=GT, h=HP)
                ch.link(ve.reciprocal(rden[:, :, :], pvT[:, :, :, HD]))
                ve.tensor_tensor(attn[:, :, HP * HD * u:HP * HD * (u + 1)].rearrange("p q (h d) -> p q h d", d=HD),
                                 pvT[:, :, :, 0:HD], rden[:, :, :].unsqueeze(3).broadcast_to([P, GT, HP, HD]),
                                 ALU.mult).then_inc(attn_ready, 1)

            def take_attnT(blocks):
                dve.wait_ge(attnT_done, blocks)
                ve.tensor_copy(attnT[:, :], FF).then_inc(attnT_ready, 1)

            def relu(n_done):
                dve.wait_ge(hg_ready, n_done)
                ve.tensor_scalar(hn[:, :], hn[:, :], 0.0, None, ALU.max).then_inc(hr_ready, 1)

            def take_hT(n_done):
                dve.wait_ge(hT_done, n_done)
                ve.tensor_copy(hT[:, :], FF).then_inc(hT_ready, 1)

            def add_bias(blocks):
                dve.wait_ge(proj_done, blocks)
                ve.tensor_tensor(s_t[:, :].rearrange("p (t d) -> p t d", d=D), FF.rearrange("p (t d) -> p t d", d=D),
                                 bproj.unsqueeze(1).broadcast_to([P, GT, D]), ALU.add).then_inc(proj_taken, 1)

            def finish(i, blocks, ch, stored_before):
                cols = bass.ds(i * GW, GW)
                dve.wait_ge(proj_taken, blocks)
                ch.link(ve.tensor_tensor(s_t[:, :], s_t[:, :], gate[:, cols], ALU.mult))
                if stored_before:
                    dve.wait_ge(out_stored, (blocks - 1) * 16)
                ve.tensor_tensor(o_sb[:, :], s_t[:, :], x_sb[:, cols], ALU.add).then_inc(out_ready, 1)

            def take_late(g, u):
                dve.wait_ge(lateT_done, UT * (g - EARLY) + u + 1)
                dve.wait_ge(stored[g % 2], STORES * (g // 2))
                ve.tensor_copy(splitT[:, g % 2, :, P * u:P * (u + 1)], late_ps).then_inc(lateT_taken, 1)

            def one_block(i, ch, first, second):
                for u in range(NU):
                    n = i * NU + u
                    head = first and u == 0
                    before = (i if u else i - 1, (u - 1) % NU)
                    if not head:
                        take_pv(n)
                        take_y(n, ch)
                        centre_y(ch)
                    take_h(n + 1, ch)
                    if head:
                        gate_ranks()
                        residue(EARLY)
                    dve.wait_ge(rs1_ready, n + 1)
                    normalize(hn, h1, mv1, rs1, hn_ready)
                    if head:
                        lo_part(EARLY)
                        rms_apply(EARLY + 1)
                    else:
                        divide(n, (u - 1) % NU, ch)
                        mix(n, ch)
                    if first:
                        take_late(EARLY + u, 0)
                    if u == 0 and not first:
                        take_attnT(i)
                    relu(n + 1)
                    if first:
                        take_late(EARLY + u, 1)
                    if first and u + 1 < LATE:
                        residue(EARLY + u + 1)
                    if u == 1 and not first:
                        add_bias(i)
                        finish(i - 1, i, ch, not second)
                    take_hT(n + 1)
                    if head:
                        gate_weights()
                    else:
                        silu(*before, n, ch)
                    if first and u + 1 < LATE:
                        lo_part(EARLY + u + 1)
                    if first and u + 2 < LATE:
                        rms_apply(EARLY + u + 2)

            one_block(0, ch, True, False)
            one_block(1, ch, False, True)
            assert ch.n == DVE_BEFORE, ("DVE_BEFORE", ch.n)
            maxima(1)
            with dve.Fori(2, NG) as i:
                ci = Chain(dve, dve_links, (i - 2) * DVE_BLOCK + DVE_BEFORE)
                one_block(i, ci, False, False)
                assert ci.n == DVE_BLOCK, ("DVE_BLOCK", ci.n)
            ce = Chain(dve, dve_links, DVE_BEFORE + (NG - 2) * DVE_BLOCK)
            last = (NG - 1, NU - 1)
            take_y(NT, ce, take_pv)
            divide(NT, NU - 1, ce)
            centre_y(ce)
            take_attnT(NG)
            mix(NT, ce)
            add_bias(NG)
            silu(*last, NT, ce)
            finish(NG - 1, NG, ce, True)

        @block.tensor
        def _(pe):
            te = nc.tensor

            def x_transpose(g):
                pe.wait_ge(xn_ready, g + 1)
                if g >= 2:
                    pe.wait_ge(xnT_ready, g - 1)
                for u in range(UT):
                    t = UT * g + u
                    last = te.transpose(xT_ps(g)[:, P * u:P * (u + 1)], xn[:, D * t:D * (t + 1)], ident[:, :])
                last.then_inc(xT_done, 1)

            def qkv(g):
                pe.wait_ge(xnT_ready, g + 1)
                if g >= 2:
                    pe.wait_ge(qk_ready, g - 1)
                    pe.wait_ge(v_taken, g - 1)
                for u in range(UT):
                    t = UT * g + u
                    last = te.matmul(qkv_ps(g)[:, u, 0:WCAT], xnT[:, P * t:P * (t + 1)], wcat_sb[:, :],
                                     start=True, stop=True)
                last.then_inc(qkv_done, 1)

            def parts_transpose(g):
                pe.wait_ge(lo_ready, g + 1)
                if g:
                    pe.wait_ge(partsT_act, g)
                    pe.wait_ge(partsT_dve, g)
                for s in range(2 * PARTS):
                    qk, part = s // PARTS, s % PARTS
                    for u in range(UT):
                        last = te.transpose(parts_ps[:, s, u, :], split[:, g % 2, part, u, D * qk:D * (qk + 1)],
                                            ident16[:, :])
                last.then_inc(partsT_done, 1)

            pe.wait_ge(ident_ready, 1)
            x_transpose(0)
            pe.wait_ge(in_w, 32)
            qkv(0)
            x_transpose(1)
            qkv(1)
            for g in range(EARLY):
                if g + 2 < EARLY:
                    x_transpose(g + 2)
                    qkv(g + 2)
                if g == EARLY - 1:
                    x_transpose(EARLY)
                    qkv(EARLY)
                    x_transpose(EARLY + 1)
                parts_transpose(g)
            qkv(EARLY + 1)
            x_transpose(EARLY + 2)
            x_transpose(EARLY + 3)
            qkv(EARLY + 2)
            qkv(EARLY + 3)
            large_scores = scores_may_be_large(pe)
            pe.wait_ge(qk_ready, NUNIT)
            pe.wait_ge(v_taken, NUNIT)
            pe.wait_ge(partsT_act, EARLY)
            pe.wait_ge(partsT_dve, EARLY)
            pe.wait_ge(in_wb, 64)

            def max_scores(b):
                with pe.If(large_scores):
                    with pe.Fori(GB * b, GB * (b + 1)) as i:
                        for u in range(NU):
                            pe.wait_ge(max_operands_in, (i * NU + u + 1) * LOADS)
                            for m in range(MAXN):
                                head, q = m // GT, m % GT
                                pe.wait_ge(max_taken, (i * NU + u) * MAXN + m - 1 + CREDIT)
                                for j in range(2):
                                    last = te.matmul(bank(2 * (m % 2) + j), q_op[:, 0, head, P * q:P * (q + 1)],
                                                     k_op[:, 0, head, GW * j:GW * (j + 1)], start=True, stop=True)
                                last.then_inc(max_scores_done, 1)
                    pe.wait_ge(shift_ready, b + 1)
                    for t in range(KT):
                        last = te.transpose(psum[0:H * PARTS, 0:GW].bitcast(BF16)[:, P * t:P * (t + 1)],
                                            shift[:, KT * b + t, :, :].rearrange("p s h -> p (s h)"), ident16[:, :])
                    last.then_inc(shiftT_done, 1)
                    pe.wait_ge(shift_rows_ready, b + 1)
                    if b == 0:
                        pe.wait_ge(first_again_in, LOADS)

            def scores(i, u, t, hp, first):
                k = u * STEPS + 2 * t + hp
                back = next(m for m in range(1, 5) if SBUF_OF[k - m] == SBUF_OF[k])
                if not (first and k < back):
                    pe.wait_ge(probs_ready, i * NU * STEPS + k - back + 1)
                for j in range(2):
                    h = 2 * hp + j
                    last = te.matmul(bank(2 * SBUF_OF[k] + j), k_op[:, u % 2, h, P * t:P * (t + 1)],
                                     q_op[:, u % 2, h, :], start=True, stop=True)
                last.then_inc(scores_done, 1)

            def values(i, u, t, first):
                k = u * STEPS + 2 * t
                pe.wait_ge(probs_ready, i * NU * STEPS + k + 2)
                if t == 0:
                    pe.wait_ge(staged, (i * NU + u) * 2 + 2)
                    if not (first and u == 0):
                        pe.wait_ge(pv_taken, i * NU + u)
                for j in range(HP):
                    last = te.matmul(PV[VW * j:VW * (j + 1), :], v_op[:, u % 2, t, j, :],
                                     probs[:, (k + j // 2) % RING, GW * (j % 2):GW * (j % 2 + 1)],
                                     start=(t == 0), stop=(t == KT - 1))
                last.then_inc(pv_done, 1)

            def mm1(i, u, first):
                n = i * NU + u
                pe.wait_ge(staged, n * 2 + 2)
                if not (first and u == 0):
                    pe.wait_ge(y_taken, n)
                te.matmul(FF, xT_op[:, u % 2, :], w1_sb[:, :], start=True, stop=True).then_inc(mm1_done, 1)

            def pv_transpose(passes):
                pe.wait_ge(pv_taken, passes)
                for q in range(GT):
                    last = te.transpose(FF[:, P * q:P * (q + 1)], pv_sb[:, P * q:P * (q + 1)], ident[:, :])
                last.then_inc(pvT_done, 1)

            def attn_transpose(passes):
                pe.wait_ge(attn_ready, passes)
                for q in range(GT):
                    last = te.transpose(FF[:, P * q:P * (q + 1)], attn[:, q, :], ident[:, :])
                last.then_inc(attnT_done, 1)

            def h_transpose(i, u, first):
                n = i * NU + u
                pe.wait_ge(hr_ready, n + 1)
                if first:
                    pe.wait_ge(lateT_taken, UT * (u + 1))
                elif u == 0:
                    pe.wait_ge(attnT_ready, i)
                elif u == 1:
                    pe.wait_ge(proj_taken, i)
                else:
                    pe.wait_ge(attn_ready, n)
                for e in range(NE):
                    last = te.transpose(FF[:, P * e:P * (e + 1)], hn[:, D * e:D * (e + 1)], ident[:, :])
                last.then_inc(hT_done, 1)

            def late_transpose(g, u):
                if u:
                    pe.wait_ge(lateT_taken, UT * (g - EARLY) + u)
                elif g == EARLY:
                    pe.wait_ge(h1_taken, 1)
                else:
                    pe.wait_ge(attn_ready, g - EARLY)
                pe.wait_ge(lo_ready, g + 1)
                for s in range(2 * PARTS):
                    qk, part = s // PARTS, s % PARTS
                    last = te.transpose(late_ps[:, s, :], split[:, g % 2, part, u, D * qk:D * (qk + 1)], ident16[:, :])
                last.then_inc(lateT_done, 1)

            def mm2(done):
                pe.wait_ge(hT_ready, done)
                for e in range(NE):
                    last = te.matmul(FF[:, D * e:D * (e + 1)], hT[:, P * e:P * (e + 1)], w2_sb[:, D * e:D * (e + 1)],
                                     start=True, stop=True)
                last.then_inc(mm2_done, 1)

            def project(blocks):
                pe.wait_ge(attnT_ready, blocks)
                for q in range(GT):
                    last = te.matmul(FF[:, D * q:D * (q + 1)], attnT[:, P * q:P * (q + 1)], wproj_sb[:, :],
                                     start=True, stop=True)
                last.then_inc(proj_done, 1)

            def one_block(i, first):
                for u in range(NU):
                    n = i * NU + u
                    if not (first and u == 0):
                        pe.wait_ge(operands_in[u % 2],
                                   i * (LOADS * NU // 2) + LOADS * (u // 2 + 1) - (LOADS if u % 2 == 0 else 0))
                    for t in range(KT):
                        if first and u == 0 and t == 0:
                            pe.wait_ge(first_q_in, 16 * PARTS)
                        if first and u == 0 and t % (KT // 2) == 0:
                            pe.wait_ge(first_k_in[t // (KT // 2)], 16 * PARTS)
                        scores(i, u, t, 0, first)
                        scores(i, u, t, 1, first)
                        if t == KT - 1:
                            h_transpose(i, u, first)
                        if t >= 2:
                            values(i, u, t - 2, first)
                        elif u:
                            values(i, u - 1, KT - 2 + t, first)
                        elif not first:
                            values(i - 1, NU - 1, KT - 2 + t, False)
                        if t == 1 and not (first and u == 0):
                            mm2(n)
                        if t == (0 if first and u == 0 else 2):
                            mm1(i, u, first)
                        if t == 3 and not (first and u == 0):
                            pe.wait_ge(h1_taken, n + 1)
                            pv_transpose(n)
                        if first and t == 5:
                            late_transpose(EARLY + u, 0)
                        if first and t == 6:
                            late_transpose(EARLY + u, 1)
                        if t == 5 and u == 0 and not first:
                            attn_transpose(n)
                        if t == 5 and u == 1 and not first:
                            pe.wait_ge(attn_ready, n)
                            project(i)

            max_scores(0)
            one_block(0, True)
            one_block(1, False)
            pe.wait_ge(probs_ready, GB * NU * STEPS)
            max_scores(1)
            with pe.Fori(2, NG) as i:
                one_block(i, False)
            mm2(NT)
            for t in (KT - 2, KT - 1):
                values(NG - 1, NU - 1, t, False)
            pe.wait_ge(y_taken, NT)
            pv_transpose(NT)
            attn_transpose(NT)
            project(NG)


_OUTS = [((B, S, D), "float32")]


def kernel(L0_attn_x, L0_attn_Wqkv, L0_attn_bqkv, L0_attn_Wproj, L0_attn_bproj, L0_attn_qn_w, L0_attn_kn_w,
           L0_ffn_gate_W, L0_ffn_gate_b, L0_ffn_W1, L0_ffn_b1, L0_ffn_g1, L0_ffn_be1, L0_ffn_W2, L0_ffn_b2,
           L0_ffn_g2, L0_ffn_be2):
    import concourse.bacc as bacc
    from concourse.bass_utils import run_bass_kernel_spmd

    def flat(*arrays):
        return np.concatenate([np.asarray(a).reshape(1, -1) for a in arrays], axis=1)

    wide = {
        "x": np.asarray(L0_attn_x),
        "wcat": np.concatenate([np.asarray(L0_attn_Wqkv).T, np.asarray(L0_ffn_gate_W)], axis=1),
        "w1": np.asarray(L0_ffn_W1).transpose(1, 0, 2).reshape(D, NE * D),
        "w2": np.asarray(L0_ffn_W2).transpose(1, 0, 2).reshape(D, NE * D),
        "wproj": np.asarray(L0_attn_Wproj).T,
        "row_a": flat(L0_attn_bqkv, L0_ffn_gate_b, L0_attn_qn_w, L0_attn_kn_w),
        "row_b": flat(L0_ffn_b1, L0_ffn_g1, L0_ffn_be1, L0_ffn_b2, L0_ffn_g2, L0_ffn_be2, L0_attn_bproj),
    }
    nc = bacc.Bacc("TRN2", target_bir_lowering=False, num_devices=1)
    arrays, args = {}, {}
    for name, a in wide.items():
        a = np.ascontiguousarray(a)
        arrays[f"in_{name}"] = a
        args[name] = nc.dram_tensor(f"in_{name}", a.shape, mybir.dt.from_np(a.dtype), kind="ExternalInput").ap()
    shape, dtype = _OUTS[0]
    out = nc.dram_tensor("out_0", shape, mybir.dt.from_np(np.dtype(dtype)), kind="ExternalOutput").ap()
    build(nc, out=out, **args)
    r = run_bass_kernel_spmd(nc, [arrays], core_ids=[0])
    return r.results[0]["out_0"]
```
